# Optimizing a Trainium2 kernel written in Bass

```python
import numpy as np
import jax
import jax.numpy as jnp

def _softmax(x, axis=-1):
    return jax.nn.softmax(x, axis=axis)

def _gelu(x):
    return jax.nn.gelu(x, approximate=True)

def _silu(x):
    return jax.nn.silu(x)

def _sigmoid(x):
    return jax.nn.sigmoid(x)

def _layernorm(x, axis=-1, eps=1e-05):
    m = jnp.mean(x, axis=axis, keepdims=True)
    v = jnp.var(x, axis=axis, keepdims=True)
    return (x - m) / jnp.sqrt(v + eps)

def _scatter_add(tgt, idx, src, axis=0):
    return tgt.at[idx].add(src)

def _segment_sum(src, seg, n):
    return jax.ops.segment_sum(src, seg, n)
kernel_name = 'mk_gnn_preln_d4_gnn_r16_1abbb4'

def setup_inputs(seed: int=0):
    np.random.seed(seed)
    _w = jnp.asarray

    def _rec_inputs():
        import jax
        import jax.numpy as jnp
        _gk = jax.random.key(seed)
        x = -0.000202 + 1 * jax.random.normal(jax.random.fold_in(_gk, 1), (3125, 128), jnp.float32)
        src = jax.random.randint(jax.random.fold_in(_gk, 2), (100000,), 0, 3125, jnp.int32)
        dst = jnp.minimum((3125 * jax.random.uniform(jax.random.fold_in(_gk, 3), (100000,)) ** 2.0).astype(jnp.int32), 49999)
        _o = jnp.argsort(dst, stable=True)
        src = src[_o]
        dst = dst[_o]
        edge_attr_64 = 0.000155561 + 1.00019 * jax.random.normal(jax.random.fold_in(_gk, 11), (100000, 64), jnp.float32)
        edge_weight = jax.random.uniform(jax.random.fold_in(_gk, 13), (100000,), jnp.float32, 0.0, 0.999998)
        return (x, src, dst, edge_attr_64, edge_weight)
    x, src, dst, edge_attr_64, edge_weight = _rec_inputs()

    def _L0_gnn_setup():
        import jax, jax.numpy as jnp
        import numpy as np
        N = 3125
        E = 100000
        D = 128
        L = 3
        EPS = 1e-05
        SLOPE = 0.2

        def _gat_forward(x, src, dst, W, a_src, a_dst, b):
            z = x
            for l in range(L):
                h = z @ W[l]
                e = jax.nn.leaky_relu((h @ a_src[l])[src] + (h @ a_dst[l])[dst], SLOPE)
                m = jax.lax.stop_gradient(jax.ops.segment_max(e, dst, num_segments=N))
                p = jnp.exp(e - m[dst])
                s = jax.ops.segment_sum(p, dst, num_segments=N)
                alpha = p / s[dst]
                z = jax.ops.segment_sum(alpha[:, None] * h[src], dst, num_segments=N) + b[l]
                mu = jnp.mean(z, axis=0)
                var = jnp.var(z, axis=0)
                z = jax.nn.relu((z - mu) * jax.lax.rsqrt(var + EPS))
            return z
        key = jax.random.key(seed)
        ks = jax.random.split(key, 5)
        x = jax.random.normal(ks[0], (N, D), jnp.float32)
        edge_index = jax.random.randint(ks[1], (2, E), 0, N)
        W = jax.random.normal(ks[2], (L, D, D), jnp.float32) * 0.1
        a_src = jax.random.normal(ks[3], (L, D), jnp.float32) * 0.1
        a_dst = jax.random.normal(ks[4], (L, D), jnp.float32) * 0.1
        b = jnp.zeros((L, D), jnp.float32)
        return {'x': x, 'edge_index': edge_index, 'W': W, 'a_src': a_src, 'a_dst': a_dst, 'b': b}
    _L0_gnn_all = _L0_gnn_setup()
    _L0_gnn_in = {k: v for k, v in _L0_gnn_all.items() if k in ('W', 'a_src', 'a_dst', 'b')}
    del _L0_gnn_all

    def _L1_gnn_setup():
        import jax, jax.numpy as jnp
        import numpy as np
        HIDDEN = 128
        EDGE_DIM = 64
        N_NODES = 3125
        N_EDGES = 37500

        def _linear_params(key, fan_in, fan_out):
            kw, kb = jax.random.split(key)
            bound = 1.0 / np.sqrt(fan_in)
            W = jax.random.uniform(kw, (fan_in, fan_out), minval=-bound, maxval=bound, dtype=jnp.float32)
            b = jax.random.uniform(kb, (fan_out,), minval=-bound, maxval=bound, dtype=jnp.float32)
            return (W, b)
        key = jax.random.key(seed)
        ks = jax.random.split(key, 10)
        h = jax.random.normal(ks[0], (N_NODES, HIDDEN), dtype=jnp.float32)
        edge_index = jax.random.randint(ks[1], (2, N_EDGES), 0, N_NODES, dtype=jnp.int64)
        edge_attr = jax.random.normal(ks[2], (N_EDGES, EDGE_DIM), dtype=jnp.float32)
        mW1, mb1 = _linear_params(ks[3], 2 * HIDDEN + EDGE_DIM, HIDDEN)
        mW2, mb2 = _linear_params(ks[4], HIDDEN, HIDDEN)
        mW3, mb3 = _linear_params(ks[5], HIDDEN, HIDDEN)
        uW1, ub1 = _linear_params(ks[6], 2 * HIDDEN, HIDDEN)
        uW2, ub2 = _linear_params(ks[7], HIDDEN, HIDDEN)
        gamma = jnp.ones((HIDDEN,), dtype=jnp.float32)
        beta = jnp.zeros((HIDDEN,), dtype=jnp.float32)
        return {'h': h, 'edge_index': edge_index, 'edge_attr': edge_attr, 'mW1': mW1, 'mb1': mb1, 'mW2': mW2, 'mb2': mb2, 'mW3': mW3, 'mb3': mb3, 'uW1': uW1, 'ub1': ub1, 'uW2': uW2, 'ub2': ub2, 'gamma': gamma, 'beta': beta}
    _L1_gnn_all = _L1_gnn_setup()
    _L1_gnn_in = {k: v for k, v in _L1_gnn_all.items() if k in ('mW1', 'mb1', 'mW2', 'mb2', 'mW3', 'mb3', 'uW1', 'ub1', 'uW2', 'ub2', 'gamma', 'beta')}
    del _L1_gnn_all

    def _L2_gnn_setup():
        import jax, jax.numpy as jnp
        import numpy as np
        N = 3125
        E = 37500
        D = 128
        H = 4
        HD = 32
        NEG = 0.2
        EPS = 1e-05

        def _gat_layer(h, src, dst, Wl, bl, Wr, br, att, bias, g, b):
            xl = (h @ Wl + bl).reshape(N, H, HD)
            xr = (h @ Wr + br).reshape(N, H, HD)
            e = jax.nn.leaky_relu(xl[src] + xr[dst], NEG)
            score = jnp.einsum('ehd,hd->eh', e, att)
            m = jax.ops.segment_max(score, dst, num_segments=N)
            m = jnp.where(jnp.isfinite(m), m, 0.0)
            ex = jnp.exp(score - m[dst])
            den = jax.ops.segment_sum(ex, dst, num_segments=N)
            alpha = ex / (den[dst] + 1e-16)
            out = jax.ops.segment_sum(alpha[:, :, None] * xl[src], dst, num_segments=N)
            out = out.reshape(N, H * HD) + bias
            mu = out.mean(-1, keepdims=True)
            var = out.var(-1, keepdims=True)
            out = (out - mu) / jnp.sqrt(var + EPS) * g + b
            return jax.nn.elu(out)
        key = jax.random.key(seed)
        ks = jax.random.split(key, 4)
        inp = {'x': jax.random.normal(ks[0], (N, D), jnp.float32), 'edge_index': jax.random.randint(ks[1], (2, E), 0, N, dtype=jnp.int32)}
        glorot = 1.0 / np.sqrt(D)
        for i in range(2):
            k = jax.random.split(jax.random.fold_in(ks[2], i), 8)
            inp[f'Wl{i}'] = jax.random.normal(k[0], (D, H * HD), jnp.float32) * glorot
            inp[f'bl{i}'] = jnp.zeros((H * HD,), jnp.float32)
            inp[f'Wr{i}'] = jax.random.normal(k[1], (D, H * HD), jnp.float32) * glorot
            inp[f'br{i}'] = jnp.zeros((H * HD,), jnp.float32)
            inp[f'att{i}'] = jax.random.normal(k[2], (H, HD), jnp.float32) * (1.0 / np.sqrt(HD))
            inp[f'bias{i}'] = jnp.zeros((H * HD,), jnp.float32)
            inp[f'g{i}'] = jnp.ones((H * HD,), jnp.float32)
            inp[f'b{i}'] = jnp.zeros((H * HD,), jnp.float32)
        return inp
    _L2_gnn_all = _L2_gnn_setup()
    _L2_gnn_in = {k: v for k, v in _L2_gnn_all.items() if k in ('Wl0', 'bl0', 'Wr0', 'br0', 'att0', 'bias0', 'g0', 'b0', 'Wl1', 'bl1', 'Wr1', 'br1', 'att1', 'bias1', 'g1', 'b1')}
    del _L2_gnn_all

    def _L3_gnn_setup():
        import jax, jax.numpy as jnp
        import numpy as np
        N = 3125
        E = 50000
        D = 128

        def _layernorm(h, gamma, beta, eps=1e-05):
            mu = jnp.mean(h, axis=-1, keepdims=True)
            var = jnp.var(h, axis=-1, keepdims=True)
            return (h - mu) * jax.lax.rsqrt(var + eps) * gamma + beta

        def _gcn_conv(h, row, col, norm, W, b):
            h = h @ W
            msg = h[row] * norm[:, None]
            agg = jax.ops.segment_sum(msg, col, num_segments=N)
            return agg + b
        key = jax.random.key(seed)
        ks = jax.random.split(key, 6)
        x = jax.random.normal(ks[0], (N, D), dtype=jnp.float32)
        edge_index = jax.random.randint(ks[1], (2, E), 0, N, dtype=jnp.int64)
        edge_weight = jax.random.uniform(ks[2], (E,), dtype=jnp.float32)
        s = 1.0 / np.sqrt(D)
        W1 = jax.random.normal(ks[3], (D, D), dtype=jnp.float32) * s
        W2 = jax.random.normal(ks[4], (D, D), dtype=jnp.float32) * s
        return {'x': x, 'edge_index': edge_index, 'edge_weight': edge_weight, 'W1': W1, 'b1': jnp.zeros((D,), jnp.float32), 'g1': jnp.ones((D,), jnp.float32), 'be1': jnp.zeros((D,), jnp.float32), 'W2': W2, 'b2': jnp.zeros((D,), jnp.float32), 'g2': jnp.ones((D,), jnp.float32), 'be2': jnp.zeros((D,), jnp.float32)}
    _L3_gnn_all = _L3_gnn_setup()
    _L3_gnn_in = {k: v for k, v in _L3_gnn_all.items() if k in ('W1', 'b1', 'g1', 'be1', 'W2', 'b2', 'g2', 'be2')}
    del _L3_gnn_all
    return {'x': x, 'src': src, 'dst': dst, 'edge_attr_64': edge_attr_64, 'edge_weight': edge_weight, 'L0_gnn_W': _L0_gnn_in['W'], 'L0_gnn_a_src': _L0_gnn_in['a_src'], 'L0_gnn_a_dst': _L0_gnn_in['a_dst'], 'L0_gnn_b': _L0_gnn_in['b'], 'L1_gnn_mW1': _L1_gnn_in['mW1'], 'L1_gnn_mb1': _L1_gnn_in['mb1'], 'L1_gnn_mW2': _L1_gnn_in['mW2'], 'L1_gnn_mb2': _L1_gnn_in['mb2'], 'L1_gnn_mW3': _L1_gnn_in['mW3'], 'L1_gnn_mb3': _L1_gnn_in['mb3'], 'L1_gnn_uW1': _L1_gnn_in['uW1'], 'L1_gnn_ub1': _L1_gnn_in['ub1'], 'L1_gnn_uW2': _L1_gnn_in['uW2'], 'L1_gnn_ub2': _L1_gnn_in['ub2'], 'L1_gnn_gamma': _L1_gnn_in['gamma'], 'L1_gnn_beta': _L1_gnn_in['beta'], 'L2_gnn_Wl0': _L2_gnn_in['Wl0'], 'L2_gnn_bl0': _L2_gnn_in['bl0'], 'L2_gnn_Wr0': _L2_gnn_in['Wr0'], 'L2_gnn_br0': _L2_gnn_in['br0'], 'L2_gnn_att0': _L2_gnn_in['att0'], 'L2_gnn_bias0': _L2_gnn_in['bias0'], 'L2_gnn_g0': _L2_gnn_in['g0'], 'L2_gnn_b0': _L2_gnn_in['b0'], 'L2_gnn_Wl1': _L2_gnn_in['Wl1'], 'L2_gnn_bl1': _L2_gnn_in['bl1'], 'L2_gnn_Wr1': _L2_gnn_in['Wr1'], 'L2_gnn_br1': _L2_gnn_in['br1'], 'L2_gnn_att1': _L2_gnn_in['att1'], 'L2_gnn_bias1': _L2_gnn_in['bias1'], 'L2_gnn_g1': _L2_gnn_in['g1'], 'L2_gnn_b1': _L2_gnn_in['b1'], 'L3_gnn_W1': _L3_gnn_in['W1'], 'L3_gnn_b1': _L3_gnn_in['b1'], 'L3_gnn_g1': _L3_gnn_in['g1'], 'L3_gnn_be1': _L3_gnn_in['be1'], 'L3_gnn_W2': _L3_gnn_in['W2'], 'L3_gnn_b2': _L3_gnn_in['b2'], 'L3_gnn_g2': _L3_gnn_in['g2'], 'L3_gnn_be2': _L3_gnn_in['be2']}

def reference(x, src, dst, edge_attr_64, edge_weight, L0_gnn_W, L0_gnn_a_src, L0_gnn_a_dst, L0_gnn_b, L1_gnn_mW1, L1_gnn_mb1, L1_gnn_mW2, L1_gnn_mb2, L1_gnn_mW3, L1_gnn_mb3, L1_gnn_uW1, L1_gnn_ub1, L1_gnn_uW2, L1_gnn_ub2, L1_gnn_gamma, L1_gnn_beta, L2_gnn_Wl0, L2_gnn_bl0, L2_gnn_Wr0, L2_gnn_br0, L2_gnn_att0, L2_gnn_bias0, L2_gnn_g0, L2_gnn_b0, L2_gnn_Wl1, L2_gnn_bl1, L2_gnn_Wr1, L2_gnn_br1, L2_gnn_att1, L2_gnn_bias1, L2_gnn_g1, L2_gnn_b1, L3_gnn_W1, L3_gnn_b1, L3_gnn_g1, L3_gnn_be1, L3_gnn_W2, L3_gnn_b2, L3_gnn_g2, L3_gnn_be2):
    import jax
    import jax.numpy as jnp

    def _L0_gnn_ref(x, edge_index, W, a_src, a_dst, b):
        import jax, jax.numpy as jnp
        import numpy as np
        N = 3125
        E = 100000
        D = 128
        L = 3
        EPS = 1e-05
        SLOPE = 0.2

        def _gat_forward(x, src, dst, W, a_src, a_dst, b):
            z = x
            for l in range(L):
                h = z @ W[l]
                e = jax.nn.leaky_relu((h @ a_src[l])[src] + (h @ a_dst[l])[dst], SLOPE)
                m = jax.lax.stop_gradient(jax.ops.segment_max(e, dst, num_segments=N))
                p = jnp.exp(e - m[dst])
                s = jax.ops.segment_sum(p, dst, num_segments=N)
                alpha = p / s[dst]
                z = jax.ops.segment_sum(alpha[:, None] * h[src], dst, num_segments=N) + b[l]
                mu = jnp.mean(z, axis=0)
                var = jnp.var(z, axis=0)
                z = jax.nn.relu((z - mu) * jax.lax.rsqrt(var + EPS))
            return z
        loops = jnp.arange(N, dtype=edge_index.dtype)
        src = jnp.concatenate([edge_index[0], loops])
        dst = jnp.concatenate([edge_index[1], loops])
        return _gat_forward(x, src, dst, W, a_src, a_dst, b)

    def _L1_gnn_ref(h, edge_index, edge_attr, mW1, mb1, mW2, mb2, mW3, mb3, uW1, ub1, uW2, ub2, gamma, beta):
        import jax, jax.numpy as jnp
        import numpy as np
        HIDDEN = 128
        EDGE_DIM = 64
        N_NODES = 3125
        N_EDGES = 37500

        def _linear_params(key, fan_in, fan_out):
            kw, kb = jax.random.split(key)
            bound = 1.0 / np.sqrt(fan_in)
            W = jax.random.uniform(kw, (fan_in, fan_out), minval=-bound, maxval=bound, dtype=jnp.float32)
            b = jax.random.uniform(kb, (fan_out,), minval=-bound, maxval=bound, dtype=jnp.float32)
            return (W, b)
        src, dst = (edge_index[0], edge_index[1])
        x = jnp.concatenate([h[src], h[dst], edge_attr], axis=-1)
        x = jax.nn.gelu(x @ mW1 + mb1)
        x = jax.nn.gelu(x @ mW2 + mb2)
        msgs = x @ mW3 + mb3
        agg = jax.ops.segment_sum(msgs, dst, num_segments=h.shape[0])
        count = jax.ops.segment_sum(jnp.ones((dst.shape[0], 1), dtype=h.dtype), dst, num_segments=h.shape[0])
        agg = agg / (count + 1e-08)
        u = jnp.concatenate([h, agg], axis=-1)
        u = jax.nn.gelu(u @ uW1 + ub1)
        out = u @ uW2 + ub2
        y = out + h
        mu = jnp.mean(y, axis=-1, keepdims=True)
        var = jnp.var(y, axis=-1, keepdims=True)
        return (y - mu) / jnp.sqrt(var + 1e-05) * gamma + beta

    def _L2_gnn_ref(x, edge_index, Wl0, bl0, Wr0, br0, att0, bias0, g0, b0, Wl1, bl1, Wr1, br1, att1, bias1, g1, b1):
        import jax, jax.numpy as jnp
        import numpy as np
        N = 3125
        E = 37500
        D = 128
        H = 4
        HD = 32
        NEG = 0.2
        EPS = 1e-05

        def _gat_layer(h, src, dst, Wl, bl, Wr, br, att, bias, g, b):
            xl = (h @ Wl + bl).reshape(N, H, HD)
            xr = (h @ Wr + br).reshape(N, H, HD)
            e = jax.nn.leaky_relu(xl[src] + xr[dst], NEG)
            score = jnp.einsum('ehd,hd->eh', e, att)
            m = jax.ops.segment_max(score, dst, num_segments=N)
            m = jnp.where(jnp.isfinite(m), m, 0.0)
            ex = jnp.exp(score - m[dst])
            den = jax.ops.segment_sum(ex, dst, num_segments=N)
            alpha = ex / (den[dst] + 1e-16)
            out = jax.ops.segment_sum(alpha[:, :, None] * xl[src], dst, num_segments=N)
            out = out.reshape(N, H * HD) + bias
            mu = out.mean(-1, keepdims=True)
            var = out.var(-1, keepdims=True)
            out = (out - mu) / jnp.sqrt(var + EPS) * g + b
            return jax.nn.elu(out)
        src, dst = (edge_index[0], edge_index[1])
        h = _gat_layer(x, src, dst, Wl0, bl0, Wr0, br0, att0, bias0, g0, b0)
        h = _gat_layer(h, src, dst, Wl1, bl1, Wr1, br1, att1, bias1, g1, b1)
        return h

    def _L3_gnn_ref(x, edge_index, edge_weight, W1, b1, g1, be1, W2, b2, g2, be2):
        import jax, jax.numpy as jnp
        import numpy as np
        N = 3125
        E = 50000
        D = 128

        def _layernorm(h, gamma, beta, eps=1e-05):
            mu = jnp.mean(h, axis=-1, keepdims=True)
            var = jnp.var(h, axis=-1, keepdims=True)
            return (h - mu) * jax.lax.rsqrt(var + eps) * gamma + beta

        def _gcn_conv(h, row, col, norm, W, b):
            h = h @ W
            msg = h[row] * norm[:, None]
            agg = jax.ops.segment_sum(msg, col, num_segments=N)
            return agg + b
        row, col = (edge_index[0], edge_index[1])
        deg = jax.ops.segment_sum(edge_weight, col, num_segments=N)
        dinv = jnp.where(deg > 0, jax.lax.rsqrt(jnp.maximum(deg, 1e-12)), 0.0)
        norm = dinv[row] * edge_weight * dinv[col]
        h = _gcn_conv(x, row, col, norm, W1, b1)
        h = jax.nn.relu(_layernorm(h, g1, be1))
        h = _gcn_conv(h, row, col, norm, W2, b2)
        h = jax.nn.relu(_layernorm(h, g2, be2))
        return h
    edge_index = jnp.stack([src, dst])
    h = jnp.maximum(_layernorm(x, axis=-1), 0.0)
    x = x + _L0_gnn_ref(h, edge_index, L0_gnn_W, L0_gnn_a_src, L0_gnn_a_dst, L0_gnn_b)
    h = jnp.maximum(_layernorm(x, axis=-1), 0.0)
    x = x + _L1_gnn_ref(h, edge_index, edge_attr_64, L1_gnn_mW1, L1_gnn_mb1, L1_gnn_mW2, L1_gnn_mb2, L1_gnn_mW3, L1_gnn_mb3, L1_gnn_uW1, L1_gnn_ub1, L1_gnn_uW2, L1_gnn_ub2, L1_gnn_gamma, L1_gnn_beta)
    h = jnp.maximum(_layernorm(x, axis=-1), 0.0)
    x = x + _L2_gnn_ref(h, edge_index, L2_gnn_Wl0, L2_gnn_bl0, L2_gnn_Wr0, L2_gnn_br0, L2_gnn_att0, L2_gnn_bias0, L2_gnn_g0, L2_gnn_b0, L2_gnn_Wl1, L2_gnn_bl1, L2_gnn_Wr1, L2_gnn_br1, L2_gnn_att1, L2_gnn_bias1, L2_gnn_g1, L2_gnn_b1)
    h = jnp.maximum(_layernorm(x, axis=-1), 0.0)
    x = x + _L3_gnn_ref(h, edge_index, edge_weight, L3_gnn_W1, L3_gnn_b1, L3_gnn_g1, L3_gnn_be1, L3_gnn_W2, L3_gnn_b2, L3_gnn_g2, L3_gnn_be2)
    return x

_drawn_inputs = setup_inputs


def setup_inputs(seed=0):
    import zlib

    import numpy as np

    out = dict(_drawn_inputs(seed))
    spreads = {'L0_gnn_b': (0.0, 2.0),
     'L1_gnn_gamma': (1.0, 0.2),
     'L1_gnn_beta': (0.0, 0.1),
     'L2_gnn_bl0': (0.0, 0.1),
     'L2_gnn_br0': (0.0, 2.0),
     'L2_gnn_bias0': (0.0, 0.1),
     'L2_gnn_g0': (1.0, 0.2),
     'L2_gnn_b0': (0.0, 0.1),
     'L2_gnn_bl1': (0.0, 0.1),
     'L2_gnn_br1': (0.0, 2.0),
     'L2_gnn_bias1': (0.0, 0.1),
     'L2_gnn_g1': (1.0, 0.2),
     'L2_gnn_b1': (0.0, 0.1),
     'L3_gnn_b1': (0.0, 0.1),
     'L3_gnn_g1': (1.0, 0.2),
     'L3_gnn_be1': (0.0, 0.1),
     'L3_gnn_b2': (0.0, 0.1),
     'L3_gnn_g2': (1.0, 0.2),
     'L3_gnn_be2': (0.0, 0.299)}
    factors = {'edge_attr_64': 8.0,
     'edge_weight': 99.837,
     'L1_gnn_mW1': 8.0,
     'L1_gnn_mb1': 64.0,
     'L1_gnn_mW2': 8.0,
     'L1_gnn_mb2': 64.0,
     'L1_gnn_mW3': 8.0,
     'L1_gnn_mb3': 200.0,
     'L1_gnn_ub1': 182.803,
     'L2_gnn_Wr0': 81.403,
     'L2_gnn_Wr1': 134.0,
     'L2_gnn_att1': 7.365,
     'L1_gnn_ub2': 45.137}
    for name, (base, spread) in spreads.items():
        noise = np.random.default_rng([zlib.crc32(name.encode()), seed]).standard_normal(out[name].shape)
        drawn = base * np.exp(spread * noise) if base else spread * noise
        out[name] = jnp.asarray(drawn.astype(out[name].dtype))
    for name, factor in factors.items():
        out[name] = (out[name] * factor).astype(out[name].dtype)
    return out
```

```python
import concourse.bass as bass
from concourse import mybir
from contextlib import ExitStack, contextmanager

F32 = mybir.dt.float32
I32 = mybir.dt.int32
ALU = mybir.AluOpType
ACT = mybir.ActivationFunctionType
AX = mybir.AxisListType

N = 3125
E = 100000
D = 128
P = 128
BN = 125
NB = N // BN
TG = 4
GE = TG * P
NG = (E + NB * (GE - 1)) // GE
SLOTS = NG * GE
EP = 125
EC = E // EP
EF = 64
META = 4
REC = EF + META
SC_T = 8
LD_G = 11
RING = 4
HEADS = 4
HD = D // HEADS
EPS = 1e-5
BIG = float(2 ** 100)


class Chip:
    pass


@contextmanager
def phase(nc, *names):
    sems = [nc.alloc_semaphore(name=f"{n}_{nc.next_id()}") for n in names]
    yield sems
    nc.clear_and_free_semaphores(sems)
    nc.all_engine_barrier()


def buffers(nc, ctx):
    def sb(name, shape, dt=F32):
        return ctx.enter_context(nc.sbuf_tensor(f"{name}_{nc.next_id()}", shape, dt))

    def pb(name, shape):
        return ctx.enter_context(nc.psum_tensor(f"{name}_{nc.next_id()}", shape, F32))
    return sb, pb


def chained(eng, sem):
    count = [0]

    def step(ins):
        count[0] += 1
        ins.then_inc(sem, 1)
        eng.wait_ge(sem, count[0])
        return count[0]
    return step


def wait(eng, sem, value):
    if not isinstance(value, int) or value > 0:
        eng.wait_ge(sem, value)


def group_at(i, r):
    return i + r // RING, r % RING


def pipeline(nc, eng, c, step):
    def blocks(g, n):
        if c is None:
            return [None] * n
        _, values = nc.values_load_multi_w_load_instructions(
            c.gblk[0:1, bass.ds(g, n)], engines=[eng.engine], min_val=0, max_val=NB - 1)
        return values

    def group(s, b):
        return (s // RING, s % RING, b)

    b0, b1 = blocks(0, 1)[0], blocks(1, 1)[0]
    step(None, group(0, b0))
    step(group(0, b0), group(1, b1))
    turns = (NG - 2) // RING
    with eng.Fori(0, turns) as i:
        bs = blocks(RING * i + 1, RING + 1)
        for j in range(1, RING + 1):
            step((*group_at(i, j), bs[j - 1]), (*group_at(i, j + 1), bs[j]))
    last = RING * turns + 1
    bt = [blocks(s, 1)[0] for s in range(last, NG)]
    for s in range(last, NG):
        step(group(s, bt[s - last]), group(s + 1, bt[s + 1 - last]) if s + 1 < NG else None)


def sort_edges(nc, c, src, dst, w, ea, recs):
    with ExitStack() as ctx:
        sb, pb = buffers(nc, ctx)
        FR = SLOTS // P // 8
        blank = sb("blank", [P, FR, REC])
        dst_i = sb("dst_i", [EP, EC], I32)
        src_i = sb("src_i", [EP, EC], I32)
        w_f = sb("w_f", [EP, EC])
        dst_f = sb("dst_f", [EP, EC])
        blk = sb("blk", [EP, EC])
        off = sb("off_by", [EP, EC])
        oh = sb("oh", [EP, EC])
        ones = sb("ones", [EP, EC])
        scan = sb("scan", [EP, EC])
        rank = sb("rank", [EP, EC])
        tmp_i = sb("tmp_i", [EP, EC], I32)
        pos = sb("pos", [EP, EC], I32)
        meta = sb("meta", [EP, EC, META])
        bid = sb("bid", [EP, NB])
        upper = sb("upper", [EP, EP])
        tot = sb("tot", [EP, NB])
        cnt = sb("cnt", [EP, NB])
        fl = sb("fl", [EP, NB])
        fl_i = sb("fl_i", [EP, NB], I32)
        gt = sb("gt", [EP, NB])
        gend = sb("gend", [EP, NB])
        base = sb("base", [EP, NB])
        gid = sb("gid", [1, NG])
        gsum = sb("gsum", [1, NG])
        recb = [sb(f"recb{k}", [EP, SC_T, REC]) for k in range(2)]
        idxb = [sb(f"idxb{k}", [EP, SC_T], I32) for k in range(2)]
        ps = pb("ps_cnt", [EP, 2, NB])

        with phase(nc, "edges_in", "blanked", "blank_set", "consts", "v", "bin_hot", "bin_tot", "bin_scan",
                   "bin_rank", "tot_ready", "cnt_ready", "pos_ready", "ea_in0", "ea_in1", "meta_in",
                   "idx_in", "scattered0", "scattered1", "begun") as \
                (edges_in, blanked, blank_set, consts, v, bin_hot, bin_tot, bin_scan, bin_rank, tot_ready,
                 cnt_ready, pos_ready, ea_in0, ea_in1, meta_in, idx_in, scattered0, scattered1, begun):
            ea_in, scattered = (ea_in0, ea_in1), (scattered0, scattered1)
            with nc.Block() as block:
                @block.sync
                def _(sp):
                    sp.dma_start(dst_i[:, :], dst.rearrange("(p t) -> p t", p=EP)).then_inc(edges_in, 16)
                    sp.dma_start(src_i[:, :], src.rearrange("(p t) -> p t", p=EP)).then_inc(edges_in, 16)
                    sp.dma_start(w_f[:, :], w.rearrange("(p t) -> p t", p=EP)).then_inc(edges_in, 16)
                    ea_v = ea.rearrange("(p t) f -> p t f", p=EP)
                    sp.wait_ge(blank_set, 2)
                    for k in range(8):
                        rows = P * FR
                        sp.dma_start(recs[k * rows:(k + 1) * rows, :].rearrange("(p a) f -> p a f", p=P),
                                     blank[:, :, :]).then_inc(blanked, 16)
                    with sp.Fori(0, EC // SC_T // 2) as i:
                        for k in range(2):
                            sp.wait_ge(scattered[k], i * (16 * SC_T))
                            sp.dma_start(recb[k][:, :, 0:EF], ea_v[:, bass.ds((2 * i + k) * SC_T, SC_T), :]) \
                                .then_inc(ea_in[k], 16)

                @block.gpsimd
                def _(g):
                    g.memset(blank[:, :, :], 0.0).then_inc(blank_set, 1)
                    g.wait_ge(blank_set, 1)
                    g.memset(blank[:, :, EF + 1:EF + 2], -1.0).then_inc(blank_set, 1)
                    g.memset(upper[:, :], 1.0).then_inc(consts, 1)
                    g.memset(ones[:, :], 1.0).then_inc(consts, 1)
                    g.iota(bid[:, :], [[1, NB]], base=0, channel_multiplier=0,
                           allow_small_or_imprecise_dtypes=True).then_inc(consts, 1)
                    g.iota(gid[:, :], [[1, NG]], base=0, channel_multiplier=0,
                           allow_small_or_imprecise_dtypes=True).then_inc(consts, 1)
                    g.wait_ge(consts, 4)
                    g.affine_select(out=upper[:, :], in_=upper[:, :], compare_op=ALU.is_gt, fill=0.0,
                                    base=0, pattern=[[1, EP]], channel_multiplier=-1).then_inc(consts, 1)
                    g.wait_ge(blanked, 16 * 8)
                    with g.Fori(0, EC // SC_T // 2) as i:
                        for k in range(2):
                            g.wait_ge(ea_in[k], (i + 1) * 16)
                            g.wait_ge(meta_in, 2 * i + k + 1)
                            g.wait_ge(idx_in, 2 * i + k + 1)
                            g.sem_inc(begun, 1)
                            for t in range(SC_T):
                                g.indirect_dma_start(
                                    out=recs[:, :], out_offset=bass.IndirectOffsetOnAxis(ap=idxb[k][:, t:t + 1], axis=0),
                                    in_=recb[k][:, t, :], in_offset=None).then_inc(scattered[k], 16)
                    for k in range(2):
                        g.wait_ge(scattered[k], (EC // SC_T // 2) * 16 * SC_T)

                @block.tensor
                def _(pe):
                    pe.wait_ge(consts, 5)
                    pe.wait_ge(tot_ready, 1)
                    pe.matmul(ps[:, 0, :], upper[:, :], tot[:, :], start=True, stop=True)
                    pe.matmul(ps[:, 1, :], ones[:, 0:EP], tot[:, :], start=True, stop=True).then_inc(cnt_ready, 1)

                @block.vector
                def _(ve):
                    step = chained(ve, v)
                    ve.wait_ge(edges_in, 48)
                    step(ve.tensor_copy(dst_f[:, :], dst_i[:, :]))
                    step(ve.tensor_scalar(blk[:, :], dst_f[:, :], 1.0 / BN, None, ALU.mult))
                    step(ve.tensor_copy(tmp_i[:, :], blk[:, :]))
                    step(ve.tensor_copy(blk[:, :], tmp_i[:, :]))
                    step(ve.scalar_tensor_tensor(off[:, :], blk[:, :], -float(BN), dst_f[:, :], ALU.mult, ALU.add))
                    step(ve.scalar_tensor_tensor(blk[:, :], off[:, :], 0.0, blk[:, :], ALU.is_lt, ALU.subtract))
                    step(ve.tensor_scalar(blk[:, :], blk[:, :], -1.0, None, ALU.mult))
                    step(ve.scalar_tensor_tensor(off[:, :], blk[:, :], -float(BN), dst_f[:, :], ALU.mult, ALU.add))
                    step(ve.scalar_tensor_tensor(blk[:, :], off[:, :], float(BN), blk[:, :], ALU.is_ge, ALU.add))
                    step(ve.scalar_tensor_tensor(meta[:, :, 1], blk[:, :], -float(BN), dst_f[:, :], ALU.mult, ALU.add))
                    step(ve.tensor_copy(meta[:, :, 0], src_i[:, :]))
                    step(ve.tensor_copy(meta[:, :, 2], w_f[:, :]))
                    step(ve.memset(meta[:, :, 3], 0.0))
                    ve.wait_ge(consts, 5)
                    with ve.Fori(0, NB) as b:
                        ve.wait_ge(bin_tot, b)
                        ve.tensor_scalar(oh[:, :], blk[:, :], bid[:, bass.ds(b, 1)], None, ALU.is_equal) \
                            .then_inc(bin_hot, 1)
                        ve.wait_ge(bin_hot, b + 1)
                        ve.tensor_reduce(tot[:, bass.ds(b, 1)], oh[:, :], AX.X, ALU.add).then_inc(bin_tot, 1)
                    ve.wait_ge(bin_tot, NB)
                    ve.memset(gsum[:, :], 0.0).then_inc(tot_ready, 1)
                    ve.wait_ge(tot_ready, 1)
                    ve.wait_ge(cnt_ready, 1)
                    step(ve.tensor_scalar(cnt[:, :], ps[:, 1, :], float(GE - 1), 1.0 / GE, ALU.add, ALU.mult))
                    step(ve.tensor_copy(fl_i[:, :], cnt[:, :]))
                    step(ve.tensor_copy(fl[:, :], fl_i[:, :]))
                    step(ve.tensor_tensor(gt[:, :], fl[:, :], cnt[:, :], ALU.is_gt))
                    step(ve.tensor_tensor(fl[:, :], fl[:, :], gt[:, :], ALU.subtract))
                    step(ve.tensor_tensor_scan(gend[:, :], ones[:, 0:NB], fl[:, :], 0.0, ALU.mult, ALU.add))
                    step(ve.tensor_tensor(base[:, :], gend[:, :], fl[:, :], ALU.subtract))
                    step(ve.scalar_tensor_tensor(base[:, :], base[:, :], float(GE), ps[:, 0, :], ALU.mult, ALU.add))
                    with ve.Fori(0, NB) as b:
                        ve.wait_ge(bin_rank, b)
                        ve.tensor_scalar(oh[:, :], blk[:, :], bid[:, bass.ds(b, 1)], None, ALU.is_equal) \
                            .then_inc(bin_hot, 1)
                        ve.wait_ge(bin_hot, b + (NB + 1))
                        ve.tensor_tensor_scan(scan[:, :], ones[:, :], oh[:, :], base[:, bass.ds(b, 1)],
                                              ALU.mult, ALU.add).then_inc(bin_scan, 1)
                        ve.wait_ge(bin_scan, b + 1)
                        ve.sem_inc(begun, 1)
                        ve.copy_predicated(rank[:, :], oh[:, :].bitcast(I32), scan[:, :]).then_inc(bin_rank, 1)
                    ve.wait_ge(bin_rank, NB)
                    ve.tensor_scalar(pos[:, :], rank[:, :], -1.0, None, ALU.add).then_inc(pos_ready, 1)
                    for b in range(NB - 1):
                        step(ve.scalar_tensor_tensor(gsum[:, :], gid[:, :], gend[0:1, b:b + 1], gsum[:, :],
                                                     ALU.is_ge, ALU.add))
                    step(ve.tensor_copy(c.gblk[:, :], gsum[:, :]))

                @block.scalar
                def _(act):
                    act.wait_ge(pos_ready, 1)
                    with act.Fori(0, EC // SC_T // 2) as i:
                        for k in range(2):
                            act.wait_ge(scattered[k], i * (16 * SC_T))
                            act.activation(recb[k][:, :, EF:REC], meta[:, bass.ds((2 * i + k) * SC_T, SC_T), :],
                                           ACT.Copy).then_inc(meta_in, 1)
                            act.activation(idxb[k][:, :], pos[:, bass.ds((2 * i + k) * SC_T, SC_T)],
                                           ACT.Copy).then_inc(idx_in, 1)


def load_meta(nc, c, recs):
    with ExitStack() as ctx:
        sb, pb = buffers(nc, ctx)
        rb = [sb(f"rb{k}", [P, LD_G, TG, REC]) for k in range(2)]
        rv = recs.rearrange("(g p k) f -> p g (k f)", p=P, k=TG)
        with phase(nc, "rows_in0", "rows_in1", "src_out", "dst_out", "w_out", "consts") as \
                (in0, in1, src_out, dst_out, w_out, consts):
            rows_in = (in0, in1)
            with nc.Block() as block:
                @block.sync
                def _(sp):
                    with sp.Fori(0, NG // LD_G // 2) as i:
                        for k in range(2):
                            if k == 0:
                                sp.wait_ge(src_out, 2 * i)
                                sp.wait_ge(dst_out, 2 * i)
                                sp.wait_ge(w_out, 2 * i)
                            sp.dma_start(rb[k][:, :, :, :].rearrange("p g k f -> p g (k f)"),
                                         rv[:, bass.ds((2 * i + k) * LD_G, LD_G), :]).then_inc(rows_in[k], 16)

                @block.scalar
                def _(act):
                    with act.Fori(0, NG // LD_G // 2) as i:
                        for k in range(2):
                            act.wait_ge(rows_in[k], (i + 1) * 16)
                            act.activation(c.idx[:, bass.ds((2 * i + k) * LD_G, LD_G), :], rb[k][:, :, :, EF],
                                           ACT.Copy).then_inc(src_out, 1)

                @block.vector
                def _(ve):
                    ve.memset(c.idx[:, NG:NG + RING, :], 0)
                    with ve.Fori(0, NG // LD_G // 2) as i:
                        for k in range(2):
                            ve.wait_ge(rows_in[k], (i + 1) * 16)
                            ve.tensor_copy(c.dlo[:, bass.ds((2 * i + k) * LD_G, LD_G), :], rb[k][:, :, :, EF + 1]) \
                                .then_inc(dst_out, 1)
                            ve.tensor_copy(c.wgt[:, bass.ds((2 * i + k) * LD_G, LD_G), :], rb[k][:, :, :, EF + 2]) \
                                .then_inc(w_out, 1)

                @block.gpsimd
                def _(g):
                    g.iota(c.iota[:, :], [[1, BN]], base=0, channel_multiplier=0,
                           allow_small_or_imprecise_dtypes=True)
                    g.memset(c.ones[:, :], 1.0).then_inc(consts, 1)
                    g.memset(c.ident[:, :], 0.0).then_inc(consts, 1)
                    g.wait_ge(consts, 2)
                    g.affine_select(out=c.ident[:, :], in_=c.ident[:, :], compare_op=ALU.not_equal, fill=1.0,
                                    base=0, pattern=[[-1, P]], channel_multiplier=1)


def normalise(nc, c, x, out, relu=True, scale=None, shift=None, add_to=None, elu=False):
    with ExitStack() as ctx:
        sb, pb = buffers(nc, ctx)
        stats = sb("ln_stats", [BN, NB, 6])
        mv = sb("ln_mv", [BN, NB, 2])
        rstd = sb("ln_rstd", [BN, NB])
        eps = sb("ln_eps", [BN, 1])
        shiftm = sb("ln_shiftm", [BN, NB])
        tmp = sb("ln_tmp", [BN, NB, D])
        tmp2 = sb("ln_tmp2", [BN, NB, D])
        rows = sb("ln_rows", [BN, 2, D])
        with phase(nc, "v", "rows_in", "var_ready", "std_ready", "coef_ready", "normed", "exped", "pre") as \
                (v, rows_in, var_ready, std_ready, coef_ready, normed, exped, pre):
            plain = scale is None
            fn = ACT.Relu if plain and relu else ACT.Identity
            target = out if plain and add_to is None else tmp
            with nc.Block() as block:
                @block.sync
                def _(sp):
                    if not plain:
                        sp.dma_start(rows[:, 0, :], scale.partition_broadcast(BN)).then_inc(rows_in, 16)
                        sp.dma_start(rows[:, 1, :], shift.partition_broadcast(BN)).then_inc(rows_in, 16)

                @block.scalar
                def _(act):
                    act.wait_ge(var_ready, 1)
                    act.activation(rstd[:, :], mv[:, :, 1], ACT.Sqrt, bias=eps[:, 0:1]).then_inc(std_ready, 1)
                    act.wait_ge(coef_ready, 1)
                    for b in range(NB):
                        ins = act.activation(target[:, b, :], x[:, b, :], fn, bias=shiftm[:, b:b + 1],
                                             scale=rstd[:, b:b + 1])
                    ins.then_inc(normed, 1)
                    if elu:
                        act.wait_ge(pre, 1)
                        act.activation(tmp2[:, :, :], tmp2[:, :, :], ACT.Exp).then_inc(exped, 1)

                @block.vector
                def _(ve):
                    step = chained(ve, v)
                    for b in range(NB):
                        ins = ve.bn_stats(stats[:, b, :], x[:, b, :])
                    step(ins)
                    for b in range(NB):
                        ins = ve.bn_aggr(mv[:, b, :], stats[:, b, :])
                    step(ins)
                    ve.memset(eps[:, :], EPS).then_inc(var_ready, 1)
                    ve.wait_ge(std_ready, 1)
                    step(ve.reciprocal(rstd[:, :], rstd[:, :]))
                    ve.scalar_tensor_tensor(shiftm[:, :], mv[:, :, 0], -1.0, rstd[:, :], ALU.mult, ALU.mult) \
                        .then_inc(coef_ready, 1)
                    ve.wait_ge(normed, 1)
                    if not plain:
                        ve.wait_ge(rows_in, 32)
                        step(ve.tensor_tensor(tmp[:, :, :], tmp[:, :, :],
                                              rows[:, 0:1, :].to_broadcast([BN, NB, D]), ALU.mult))
                        step(ve.tensor_tensor(tmp[:, :, :], tmp[:, :, :],
                                              rows[:, 1:2, :].to_broadcast([BN, NB, D]), ALU.add))
                    if elu:
                        ve.tensor_scalar(tmp2[:, :, :], tmp[:, :, :], 0.0, None, ALU.min).then_inc(pre, 1)
                        step(ve.tensor_scalar(tmp[:, :, :], tmp[:, :, :], 0.0, None, ALU.max))
                        ve.wait_ge(exped, 1)
                        step(ve.scalar_tensor_tensor(tmp[:, :, :], tmp2[:, :, :], -1.0, tmp[:, :, :],
                                                     ALU.add, ALU.add))
                    elif not plain and relu:
                        step(ve.tensor_scalar(tmp[:, :, :], tmp[:, :, :], 0.0, None, ALU.max))
                    if add_to is not None:
                        step(ve.tensor_tensor(add_to[:, :, :], add_to[:, :, :], tmp[:, :, :], ALU.add))
                    elif not plain:
                        step(ve.tensor_copy(out[:, :, :], tmp[:, :, :]))


def linear(nc, c, terms, width, out, addend=None, func=None, table=None, table_cols=None, row_scale=None):
    with ExitStack() as ctx:
        sb, pb = buffers(nc, ctx)
        nt = len(terms)
        xt = [[sb(f"lin_xt{t}{k}", [P, BN]) for k in range(2)] for t in range(nt)]
        pt = [pb(f"lin_pt{k}", [P, nt, 512]) for k in range(2)]
        po = [pb(f"lin_po{k}", [BN, 512]) for k in range(2)]
        with phase(nc, "turned", "turned_out", "summed", "added", "applied", "stored") as \
                (turned, turned_out, summed, added, applied, stored):
            with nc.Block() as block:
                @block.tensor
                def _(pe):
                    for s in range(NB + 1):
                        if s < NB:
                            wait(pe, turned_out, s - 1)
                            for t, (x, _) in enumerate(terms):
                                ins = pe.transpose(pt[s % 2][:, t, 0:BN], x[:, s, :], c.ident[0:BN, 0:BN])
                            ins.then_inc(turned, 1)
                        if s > 0:
                            b = s - 1
                            pe.wait_ge(turned_out, b + 1)
                            wait(pe, added, b - 1)
                            for t, (_, wt) in enumerate(terms):
                                ins = pe.matmul(po[b % 2][:, 0:width], xt[t][b % 2][:, :], wt,
                                                start=t == 0, stop=t == nt - 1)
                            ins.then_inc(summed, 1)

                @block.scalar
                def _(act):
                    for b in range(NB):
                        act.wait_ge(turned, b + 1)
                        wait(act, summed, b - 1)
                        for t in range(nt):
                            ins = act.activation(xt[t][b % 2][:, :], pt[b % 2][:, t, 0:BN], ACT.Copy)
                        ins.then_inc(turned_out, 1)
                    if func is not None:
                        act.wait_ge(added, NB)
                        for b in range(0, NB, 5):
                            ins = act.activation(out[:, b:b + 5, :], out[:, b:b + 5, :], func)
                        ins.then_inc(applied, 1)

                @block.vector
                def _(ve):
                    for b in range(NB):
                        ve.wait_ge(summed, b + 1)
                        if addend is not None:
                            ins = ve.tensor_tensor(out[:, b, 0:width], po[b % 2][:, 0:width], addend(b), ALU.add)
                        elif row_scale is not None:
                            ins = ve.tensor_scalar(out[:, b, 0:width], po[b % 2][:, 0:width], row_scale(b), None, ALU.mult)
                        else:
                            ins = ve.tensor_copy(out[:, b, 0:width], po[b % 2][:, 0:width])
                        ins.then_inc(added, 1)

                @block.sync
                def _(sp):
                    if table is not None:
                        sp.wait_ge(added, NB)
                        sp.dma_start(table.rearrange("(b p) f -> p b f", p=BN), out[:, :, 0:table_cols]) \
                            .then_inc(stored, 16)
                        sp.wait_ge(stored, 16)


def gather_rows(g, table, rows, idxb, idx_ready, rows_in, agg_done, begun):
    def gather(i, r):
        n = RING * i + r
        g.wait_ge(idx_ready, n + 1)
        wait(g, agg_done, n - RING + 1)
        g.sem_inc(begun, 1)
        for k in range(TG):
            g.indirect_dma_start(out=rows[r][:, k, :], out_offset=None, in_=table,
                                 in_offset=bass.IndirectOffsetOnAxis(ap=idxb[r][:, k:k + 1], axis=0)) \
                .then_inc(rows_in[r], 16)
    for r in range(RING):
        gather(0, r)
    with g.Fori(1, NG // RING) as i:
        for r in range(RING):
            gather(i, r)


def idx_ahead(act, c, idxb, idx_ready, rows_in, front):
    i, r, _ = front
    pi, pr = (i, r - 1) if r else (i - 1, RING - 1)
    if not isinstance(i, int) or i > 0 or r > 0:
        act.wait_ge(rows_in[pr], (pi + 1) * (16 * TG))
    act.activation(idxb[(r + RING - 1) % RING][:, :], c.idx[:, bass.ds(RING * i + r + RING - 1, 1), :], ACT.Copy) \
        .then_inc(idx_ready, 1)


def first_idx(act, c, idxb, idx_ready):
    for r in range(RING - 1):
        act.activation(idxb[r][:, :], c.idx[:, r, :], ACT.Copy).then_inc(idx_ready, 1)


def one_hot(ve, c, out, g, weight=None):
    for k in range(TG):
        dlo = c.dlo[:, bass.ds(g, 1), k]
        if weight is None:
            ins = ve.tensor_scalar(out[:, k, :], c.iota[:, :], dlo, None, ALU.is_equal)
        else:
            ins = ve.tensor_scalar(out[:, k, :], c.iota[:, :], dlo, weight(k), ALU.is_equal, ALU.mult)
    return ins


GW = 132
GA = 131


def gat_pass(nc, c, table):
    with ExitStack() as ctx:
        sb, pb = buffers(nc, ctx)
        rows = [sb(f"rows{r}", [P, TG, GW]) for r in range(RING)]
        idxb = [sb(f"idxb{r}", [P, TG], I32) for r in range(RING)]
        hot = [sb(f"hot{k}", [P, TG, BN]) for k in range(2)]
        hotp = [sb(f"hotp{k}", [P, TG, BN]) for k in range(2)]
        hott = [sb(f"hott{k}", [BN, GE]) for k in range(2)]
        pen = [sb(f"pen{k}", [BN, GE]) for k in range(2)]
        junk = sb("junk", [BN, GE])
        top = sb("top", [BN, 1])
        node = [sb(f"node{k}", [BN, 5]) for k in range(2)]
        fade = [sb(f"fade{k}", [BN, 1]) for k in range(2)]
        t = sb("t", [P, TG])
        p = sb("p", [P, TG])
        ps_hott = [pb(f"ps_hott{k}", [P, 512]) for k in range(2)]
        ps_s = [pb(f"ps_s{k}", [P, 512]) for k in range(2)]
        ps_node = [pb(f"ps_node{k}", [P, TG, 2]) for k in range(2)]
        ps_acc = [pb(f"ps_acc{k}", [BN, 512]) for k in range(2)]
        with phase(nc, "idx_ready", "in0", "in1", "in2", "in3", "hot_ready", "hott_ready", "hott_out", "pen_ready",
                   "s_ready", "top_done", "node_in", "newtop", "st_done", "y_done", "max_ready", "fade_ready",
                   "at_edges", "t1", "t2", "t3", "t_ready", "p_ready", "hotp_ready", "agg_done", "acc_done", "begun") as \
                (idx_ready, in0, in1, in2, in3, hot_ready, hott_ready, hott_out, pen_ready,
                 s_ready, top_done, node_in, newtop, st_done, y_done, max_ready, fade_ready,
                 at_edges, t1, t2, t3, t_ready, p_ready, hotp_ready, agg_done, acc_done, begun):
            rows_in = (in0, in1, in2, in3)
            with nc.Block() as block:
                @block.gpsimd
                def _(g):
                    gather_rows(g, table, rows, idxb, idx_ready, rows_in, agg_done, begun)

                @block.vector
                def _(ve):
                    def step(back, front):
                        if back:
                            i, r, b = back
                            g, k = RING * i + r, r % 2
                            ve.wait_ge(rows_in[r], (i + 1) * (16 * TG))
                            ve.wait_ge(at_edges, g + 1)
                            ve.tensor_tensor(t[:, :], rows[r][:, :, D], ps_node[k][:, :, 0], ALU.add).then_inc(t1, 1)
                            ve.wait_ge(t1, g + 1)
                            ve.scalar_tensor_tensor(t[:, :], t[:, :], 0.2, t[:, :], ALU.mult, ALU.max).then_inc(t2, 1)
                            ve.wait_ge(t2, g + 1)
                            ve.tensor_tensor(t[:, :], t[:, :], ps_node[k][:, :, 1], ALU.subtract).then_inc(t3, 1)
                            ve.wait_ge(t3, g + 1)
                            ve.tensor_scalar(t[:, :], t[:, :], 0.0, None, ALU.min).then_inc(t_ready, 1)
                        if front:
                            fi, fr, fb = front
                            fg, fk = RING * fi + fr, fr % 2
                            one_hot(ve, c, hot[fk], fg).then_inc(hot_ready, 1)
                        if back:
                            ve.wait_ge(p_ready, g + 1)
                            one_hot(ve, c, hotp[k], g, lambda q: p[:, q:q + 1]).then_inc(hotp_ready, 1)
                        if front:
                            ve.wait_ge(pen_ready, fg + 1)
                            ve.wait_ge(s_ready, fg + 1)
                            wait(ve, newtop, fg)
                            ve.sem_inc(begun, 1)
                            ve.tensor_tensor_reduce(out=junk[:, :], in0=pen[fk][:, :], in1=ps_s[fk][0:BN, :], scale=1.0,
                                                    scalar=-BIG, op0=ALU.add, op1=ALU.max, accum_out=top[:, :]) \
                                .then_inc(top_done, 1)
                            wait(ve, st_done, fg)
                            ve.tensor_scalar(node[fk][:, 0:2], c.st[:, bass.ds(fb, 1), :], 1.0, None, ALU.mult).then_inc(node_in, 1)
                            ve.wait_ge(node_in, fg + 1)
                            ve.wait_ge(top_done, fg + 1)
                            ve.tensor_tensor(node[fk][:, 2:3], node[fk][:, 1:2], top[:, :], ALU.max).then_inc(newtop, 1)
                            ve.wait_ge(newtop, fg + 1)
                            ve.tensor_scalar(c.st[:, bass.ds(fb, 1), 1], node[fk][:, 2:3], 1.0, None, ALU.mult).then_inc(st_done, 1)
                            ve.tensor_scalar(node[fk][:, 3:5], node[fk][:, 1:3], node[fk][:, 0:1], None, ALU.add) \
                                .then_inc(y_done, 1)
                            ve.wait_ge(y_done, fg + 1)
                            ve.scalar_tensor_tensor(node[fk][:, 3:5], node[fk][:, 3:5], 0.2, node[fk][:, 3:5],
                                                    ALU.mult, ALU.max).then_inc(max_ready, 1)
                        if back:
                            ve.wait_ge(agg_done, g + 1)
                            ve.wait_ge(fade_ready, g + 1)
                            wait(ve, acc_done, g)
                            ve.scalar_tensor_tensor(c.acc[:, bass.ds(b, 1), 0:GA], c.acc[:, bass.ds(b, 1), 0:GA],
                                                    fade[k][:, 0:1], ps_acc[k][:, 0:GA], ALU.mult, ALU.add) \
                                .then_inc(acc_done, 1)
                    pipeline(nc, ve, c, step)

                @block.scalar
                def _(act):
                    first_idx(act, c, idxb, idx_ready)

                    def step(back, front):
                        if back:
                            i, r, _ = back
                            g, k = RING * i + r, r % 2
                            act.wait_ge(max_ready, g + 1)
                            wait(act, acc_done, g - 1)
                            act.activation(fade[k][:, :], node[k][:, 4:5], ACT.Exp, bias=node[k][:, 3:4], scale=-1.0) \
                                .then_inc(fade_ready, 1)
                            act.wait_ge(t_ready, g + 1)
                            wait(act, hotp_ready, g)
                            act.activation(p[:, :], t[:, :], ACT.Exp).then_inc(p_ready, 1)
                        if front:
                            i, r, _ = front
                            g, k = RING * i + r, r % 2
                            act.wait_ge(hott_ready, g + 1)
                            wait(act, at_edges, g - 1)
                            act.activation(hott[k][:, :], ps_hott[k][0:BN, :], ACT.Copy).then_inc(hott_out, 1)
                            wait(act, top_done, g - 1)
                            act.activation(pen[k][:, :], ps_hott[k][0:BN, :], ACT.Copy, bias=-BIG, scale=BIG) \
                                .then_inc(pen_ready, 1)
                            idx_ahead(act, c, idxb, idx_ready, rows_in, front)
                    pipeline(nc, act, None, step)

                @block.tensor
                def _(pe):
                    def step(back, front):
                        if back:
                            i, r, _ = back
                            g, k = RING * i + r, r % 2
                            pe.wait_ge(max_ready, g + 1)
                            pe.wait_ge(hott_out, g + 1)
                            for q in range(TG):
                                ins = pe.matmul(ps_node[k][:, q, :], hott[k][:, q * P:(q + 1) * P], node[k][:, 0:5:4],
                                                start=True, stop=True)
                            ins.then_inc(at_edges, 1)
                        if front:
                            i, r, _ = front
                            fg, fk = RING * i + r, r % 2
                            pe.wait_ge(hot_ready, fg + 1)
                            wait(pe, pen_ready, fg - 1)
                            for q in range(TG):
                                ins = pe.transpose(ps_hott[fk][0:BN, q * P:(q + 1) * P], hot[fk][:, q, :], c.ident[:, :])
                            ins.then_inc(hott_ready, 1)
                            pe.wait_ge(rows_in[r], (i + 1) * (16 * TG))
                            wait(pe, top_done, fg - 1)
                            for q in range(TG):
                                ins = pe.matmul(ps_s[fk][0:BN, q * P:(q + 1) * P],
                                                rows[r][:, q, D:D + 1].to_broadcast([P, BN]), c.ident[:, :],
                                                start=True, stop=True)
                            ins.then_inc(s_ready, 1)
                        if back:
                            i, r, _ = back
                            pe.wait_ge(hotp_ready, g + 1)
                            wait(pe, acc_done, g - 1)
                            for q in range(TG):
                                ins = pe.matmul(ps_acc[k][:, 0:GA], hotp[k][:, q, :], rows[r][:, q, 0:GA],
                                                start=q == 0, stop=q == TG - 1)
                            ins.then_inc(agg_done, 1)
                    pipeline(nc, pe, None, step)


def gat_tables(nc, c, z, w, a_src, a_dst, table):
    with ExitStack() as ctx:
        sb, pb = buffers(nc, ctx)
        wx = sb("wx", [D, D + 2])
        wt = sb("wt", [D, D])
        a2 = sb("a2", [D, 2])
        pw = pb("pw", [D, D])
        pa = pb("pa", [D, 2])
        with phase(nc, "w_in", "w_turned", "w_out", "wa", "wa_out") as (w_in, w_turned, w_out, wa, wa_out):
            with nc.Block() as block:
                @block.sync
                def _(sp):
                    sp.dma_start(wx[:, 0:D], w).then_inc(w_in, 16)
                    with nc.allow_non_contiguous_dma("one column"):
                        sp.dma_start(a2[:, 0:1], a_src.rearrange("(f a) -> f a", a=1)).then_inc(w_in, 16)
                        sp.dma_start(a2[:, 1:2], a_dst.rearrange("(f a) -> f a", a=1)).then_inc(w_in, 16)

                @block.tensor
                def _(pe):
                    pe.wait_ge(w_in, 48)
                    pe.transpose(pw[:, :], wx[:, 0:D], c.ident[:, :]).then_inc(w_turned, 1)
                    pe.wait_ge(w_out, 1)
                    pe.matmul(pa[:, :], wt[:, :], a2[:, :], start=True, stop=True).then_inc(wa, 1)

                @block.vector
                def _(ve):
                    ve.memset(c.rows[:, :, 0:GW], 0.0)
                    ve.wait_ge(w_turned, 1)
                    ve.tensor_copy(wt[:, :], pw[:, :]).then_inc(w_out, 1)
                    ve.wait_ge(wa, 1)
                    ve.tensor_copy(wx[:, D:D + 2], pa[:, :]).then_inc(wa_out, 1)
                    ve.wait_ge(wa_out, 1)
                    ve.memset(c.rows[:, :, D + 2:D + 3], 1.0)
        linear(nc, c, [(z, wx[:, :])], D + 2, c.rows, table=table, table_cols=GW)
    with nc.Block() as block:
        @block.vector
        def _(ve):
            ve.tensor_copy(c.acc[:, :, 0:GW], c.rows[:, :, 0:GW])
            ve.tensor_copy(c.st[:, :, 0], c.rows[:, :, D + 1])
            ve.tensor_copy(c.st[:, :, 1], c.rows[:, :, D])


def gat_norm(nc, c, bias, out, add_to=None):
    with ExitStack() as ctx:
        sb, pb = buffers(nc, ctx)
        z = sb("z", [BN, NB, D])
        sq = sb("sq", [BN, NB, D])
        rden = sb("rden", [BN, NB])
        bias_r = sb("bias_r", [BN, 1, D])
        mean = sb("mean", [BN, 1, D])
        std = sb("std", [BN, 1, D])
        eps = sb("eps", [BN, 1])
        ps = [pb(f"ps_bn{k}", [BN, D]) for k in range(2)]
        with phase(nc, "v", "b_in", "z_ready", "mean_ready", "centred", "squared", "var_ready", "std_ready") as \
                (v, b_in, z_ready, mean_ready, centred, squared, var_ready, std_ready):
            with nc.Block() as block:
                @block.sync
                def _(sp):
                    sp.dma_start(bias_r[:, 0, :], bias.partition_broadcast(BN)).then_inc(b_in, 16)

                @block.vector
                def _(ve):
                    step = chained(ve, v)
                    full = [BN, NB, D]
                    step(ve.reciprocal(rden[:, :], c.acc[:, :, D + 2]))
                    step(ve.tensor_tensor(z[:, :, :], c.acc[:, :, 0:D], rden[:, :].unsqueeze(2).to_broadcast(full), ALU.mult))
                    ve.wait_ge(b_in, 16)
                    ve.memset(eps[:, :], EPS)
                    ve.tensor_tensor(z[:, :, :], z[:, :, :], bias_r[:, :, :].to_broadcast(full), ALU.add).then_inc(z_ready, 1)
                    ve.wait_ge(mean_ready, 1)
                    step(ve.tensor_scalar(mean[:, 0, :], ps[0][:, :], 1.0 / N, None, ALU.mult))
                    ve.tensor_tensor(z[:, :, :], z[:, :, :], mean[:, :, :].to_broadcast(full), ALU.subtract).then_inc(centred, 1)
                    ve.wait_ge(std_ready, 1)
                    step(ve.reciprocal(std[:, :, :], std[:, :, :]))
                    step(ve.tensor_tensor(z[:, :, :], z[:, :, :], std[:, :, :].to_broadcast(full), ALU.mult))
                    if add_to is None:
                        step(ve.tensor_scalar(out[:, :, :], z[:, :, :], 0.0, None, ALU.max))
                    else:
                        step(ve.scalar_tensor_tensor(add_to[:, :, :], z[:, :, :], 0.0, add_to[:, :, :], ALU.max, ALU.add))

                @block.scalar
                def _(act):
                    act.wait_ge(centred, 1)
                    act.activation(sq[:, :, :], z[:, :, :], ACT.Square).then_inc(squared, 1)
                    act.wait_ge(var_ready, 1)
                    act.activation(std[:, 0, :], ps[1][:, :], ACT.Sqrt, bias=eps[:, 0:1], scale=1.0 / N).then_inc(std_ready, 1)

                @block.tensor
                def _(pe):
                    for k, (x, ready, done) in enumerate(((z, z_ready, mean_ready), (sq, squared, var_ready))):
                        pe.wait_ge(ready, 1)
                        for b in range(NB):
                            ins = pe.matmul(ps[k][:, :], c.ones[0:BN, 0:BN], x[:, b, :], start=b == 0, stop=b == NB - 1)
                        ins.then_inc(done, 1)


def load_rows(nc, pairs):
    with phase(nc, "loaded") as (loaded,):
        with nc.Block() as block:
            @block.sync
            def _(sp):
                for dst, src in pairs:
                    sp.dma_start(dst, src).then_inc(loaded, 16)
                sp.wait_ge(loaded, 16 * len(pairs))


MA = D + 2


def mlp_pass(nc, c, table, recs, w1, b1, w2, b2):
    with ExitStack() as ctx:
        sb, pb = buffers(nc, ctx)
        rows = [sb(f"rows{r}", [P, TG, D]) for r in range(RING)]
        feat = [sb(f"feat{r}", [P, TG, EF]) for r in range(RING)]
        idxb = [sb(f"idxb{r}", [P, TG], I32) for r in range(RING)]
        hot = [sb(f"hot{k}", [P, TG, BN]) for k in range(2)]
        hott = [sb(f"hott{k}", [BN, GE]) for k in range(2)]
        featt = [sb(f"featt{k}", [EF, GE]) for k in range(2)]
        mine = [sb(f"mine{k}", [BN, D]) for k in range(2)]
        g1 = [sb(f"g1{k}", [D, GE]) for k in range(2)]
        u2 = sb("u2", [P, TG, D])
        g2 = [sb(f"g2{k}", [P, TG, MA]) for k in range(2)]
        w1c = sb("w1c", [EF, D])
        w2s = sb("w2s", [D, D])
        b1c = sb("b1c", [D, 1])
        b2r = sb("b2r", [P, 1, D])
        ps_hott = pb("ps_hott", [P, 512])
        ps_featt = pb("ps_featt", [P, 512])
        ps_1 = [pb(f"ps_1{k}", [D, 512]) for k in range(2)]
        ps_2 = [pb(f"ps_2{k}", [P, TG, D]) for k in range(2)]
        ps_acc = [pb(f"ps_acc{k}", [BN, 512]) for k in range(2)]
        rv = recs.rearrange("(g p k) f -> p g k f", p=P, k=TG)
        with phase(nc, "idx_ready", "in0", "in1", "in2", "in3", "feat0", "feat1", "feat2", "feat3", "w_in", "ones_set",
                   "hot_ready", "hott_ready", "featt_ready", "hott_out", "featt_out", "mine_ready", "sum1", "gelu1",
                   "sum2", "biased", "wcol", "gelu2", "agg_done", "acc_done", "begun") as \
                (idx_ready, in0, in1, in2, in3, feat0, feat1, feat2, feat3, w_in, ones_set,
                 hot_ready, hott_ready, featt_ready, hott_out, featt_out, mine_ready, sum1, gelu1,
                 sum2, biased, wcol, gelu2, agg_done, acc_done, begun):
            rows_in, feat_in = (in0, in1, in2, in3), (feat0, feat1, feat2, feat3)
            with nc.Block() as block:
                @block.gpsimd
                def _(g):
                    gather_rows(g, table, rows, idxb, idx_ready, rows_in, agg_done, begun)

                @block.sync
                def _(sp):
                    sp.dma_start(w1c[:, :], w1[2 * D:2 * D + EF, :]).then_inc(w_in, 16)
                    sp.dma_start(w2s[:, :], w2).then_inc(w_in, 16)
                    with nc.allow_non_contiguous_dma("one column"):
                        sp.dma_start(b1c[:, :], b1.rearrange("(f a) -> f a", a=1)).then_inc(w_in, 16)
                    sp.dma_start(b2r[:, 0, :], b2.partition_broadcast(P)).then_inc(w_in, 16)

                    def load(i, r):
                        wait(sp, featt_ready, RING * i + r - RING + 1)
                        sp.dma_start(feat[r][:, :, :], rv[:, bass.ds(RING * i + r, 1), :, 0:EF] if not isinstance(i, int)
                                     else rv[:, RING * i + r, :, 0:EF]).then_inc(feat_in[r], 16)
                    for r in range(RING):
                        load(0, r)
                    with sp.Fori(1, NG // RING) as i:
                        for r in range(RING):
                            load(i, r)

                @block.vector
                def _(ve):
                    for k in range(2):
                        ve.memset(g2[k][:, :, D:D + 1], 1.0).then_inc(ones_set, 1)
                    ve.wait_ge(w_in, 64)

                    def step(back, front):
                        if back:
                            i, r, b = back
                            g, k = RING * i + r, r % 2
                            ve.wait_ge(sum2, g + 1)
                            wait(ve, gelu2, g)
                            ve.tensor_tensor(u2[:, :, :], ps_2[k][:, :, :], b2r[:, :, :].to_broadcast([P, TG, D]), ALU.add) \
                                .then_inc(biased, 1)
                            wait(ve, agg_done, g - 1)
                            ve.tensor_scalar(g2[k][:, :, D + 1], c.wgt[:, bass.ds(g, 1), :], 1.0, None, ALU.mult).then_inc(wcol, 1)
                        if front:
                            fi, fr, fb = front
                            fg, fk = RING * fi + fr, fr % 2
                            one_hot(ve, c, hot[fk], fg).then_inc(hot_ready, 1)
                            ve.wait_ge(featt_ready, fg + 1)
                            wait(ve, sum1, fg - 1)
                            ve.tensor_copy(featt[fk][:, :], ps_featt[0:EF, :]).then_inc(featt_out, 1)
                        if back:
                            ve.wait_ge(agg_done, g + 1)
                            wait(ve, acc_done, g)
                            ve.tensor_tensor(c.acc[:, bass.ds(b, 1), 0:MA], c.acc[:, bass.ds(b, 1), 0:MA],
                                             ps_acc[k][:, 0:MA].unsqueeze(1), ALU.add).then_inc(acc_done, 1)
                    pipeline(nc, ve, c, step)

                @block.scalar
                def _(act):
                    act.wait_ge(w_in, 64)
                    first_idx(act, c, idxb, idx_ready)

                    def step(back, front):
                        if front:
                            i, r, b = front
                            g, k = RING * i + r, r % 2
                            wait(act, sum1, g - 1)
                            act.activation(mine[k][:, :], c.other[:, bass.ds(b, 1), :], ACT.Copy).then_inc(mine_ready, 1)
                            act.wait_ge(hott_ready, g + 1)
                            act.activation(hott[k][:, :], ps_hott[0:BN, :], ACT.Copy).then_inc(hott_out, 1)
                            idx_ahead(act, c, idxb, idx_ready, rows_in, front)
                        if back:
                            i, r, _ = back
                            g, k = RING * i + r, r % 2
                            act.wait_ge(biased, g + 1)
                            act.activation(g2[k][:, :, 0:D], u2[:, :, :], ACT.Gelu_apprx_tanh).then_inc(gelu2, 1)
                        if front:
                            i, r, _ = front
                            g, k = RING * i + r, r % 2
                            act.wait_ge(sum1, g + 1)
                            act.activation(g1[k][:, :], ps_1[k][:, :], ACT.Gelu_apprx_tanh, bias=b1c[:, 0:1]) \
                                .then_inc(gelu1, 1)
                    pipeline(nc, act, c, step)

                @block.tensor
                def _(pe):
                    pe.wait_ge(w_in, 64)
                    pe.wait_ge(ones_set, 2)

                    def step(back, front):
                        if back:
                            i, r, _ = back
                            g, k = RING * i + r, r % 2
                            pe.wait_ge(gelu1, g + 1)
                            wait(pe, biased, g - 1)
                            for q in range(TG):
                                ins = pe.matmul(ps_2[k][:, q, :], g1[k][:, q * P:(q + 1) * P], w2s[:, :],
                                                start=True, stop=True)
                            ins.then_inc(sum2, 1)
                        if front:
                            i, r, _ = front
                            fg, fk = RING * i + r, r % 2
                            pe.wait_ge(feat_in[r], (i + 1) * 16)
                            wait(pe, featt_out, fg)
                            for q in range(TG):
                                if q == 0:
                                    pe.sem_inc(begun, 1)
                                ins = pe.transpose(ps_featt[0:EF, q * P:(q + 1) * P], feat[r][:, q, :], c.ident[:, :])
                            ins.then_inc(featt_ready, 1)
                            pe.wait_ge(hot_ready, fg + 1)
                            wait(pe, hott_out, fg)
                            for q in range(TG):
                                ins = pe.transpose(ps_hott[0:BN, q * P:(q + 1) * P], hot[fk][:, q, :], c.ident[:, :])
                            ins.then_inc(hott_ready, 1)
                            pe.wait_ge(featt_out, fg + 1)
                            wait(pe, gelu1, fg - 1)
                            pe.matmul(ps_1[fk][:, :], w1c[:, :], featt[fk][:, :], start=True, stop=False)
                            pe.wait_ge(rows_in[r], (i + 1) * (16 * TG))
                            for q in range(TG):
                                pe.matmul(ps_1[fk][:, q * P:(q + 1) * P], rows[r][:, q, :], c.ident[:, :],
                                          start=False, stop=False)
                            pe.wait_ge(hott_out, fg + 1)
                            pe.wait_ge(mine_ready, fg + 1)
                            pe.matmul(ps_1[fk][:, :], mine[fk][:, :], hott[fk][:, :], start=False, stop=True) \
                                .then_inc(sum1, 1)
                        if back:
                            pe.wait_ge(gelu2, g + 1)
                            pe.wait_ge(wcol, g + 1)
                            wait(pe, acc_done, g - 1)
                            for q in range(TG):
                                ins = pe.matmul(ps_acc[k][:, 0:MA], hot[k][:, q, :], g2[k][:, q, :],
                                                start=q == 0, stop=q == TG - 1)
                            ins.then_inc(agg_done, 1)
                    pipeline(nc, pe, None, step)


HW = HD + 1


def gatv2_pass(nc, c, table, att):
    with ExitStack() as ctx:
        sb, pb = buffers(nc, ctx)
        rows = [sb(f"rows{r}", [P, TG, D]) for r in range(RING)]
        idxb = [sb(f"idxb{r}", [P, TG], I32) for r in range(RING)]
        hot = [sb(f"hot{k}", [P, TG, BN]) for k in range(2)]
        hott = [sb(f"hott{k}", [BN, GE]) for k in range(2)]
        pen = [sb(f"pen{k}", [BN, GE]) for k in range(2)]
        mine = [sb(f"mine{k}", [BN, D]) for k in range(2)]
        low = [sb(f"low{k}", [D, GE]) for k in range(2)]
        lr = [sb(f"lr{k}", [D, GE]) for k in range(2)]
        junk = sb("junk", [BN, GE])
        gtop = sb("gtop", [BN, HEADS])
        node = [sb(f"node{k}", [BN, 2, HEADS]) for k in range(2)]
        drop = [sb(f"drop{k}", [BN, HEADS]) for k in range(2)]
        fade = [sb(f"fade{k}", [BN, HEADS]) for k in range(2)]
        sc = [sb(f"sc{k}", [P, TG * HEADS]) for k in range(2)]
        t = sb("t", [P, TG * HEADS])
        p = sb("p", [P, TG * HEADS])
        val = [sb(f"val{k}", [P, TG * HEADS, HW]) for k in range(2)]
        faded = sb("faded", [BN, HEADS, HW])
        attc = sb("attc", [D, 1])
        att4 = sb("att4", [D, HEADS])
        attr = sb("attr", [D, HEADS, BN])
        ps_hott = pb("ps_hott", [P, 512])
        ps_e = pb("ps_e", [D, 512])
        ps_top = [pb(f"ps_top{k}", [BN, 512]) for k in range(2)]
        ps_sc = pb("ps_sc", [P, 512])
        ps_node = pb("ps_node", [P, 512])
        ps_acc = pb("ps_acc", [BN, 512])
        with phase(nc, "idx_ready", "in0", "in1", "in2", "in3", "w_in", "att_set", "att_cols", "att_ready", "hot_ready",
                   "hott_ready", "hott_out", "pen_ready", "mine_ready", "sum_e", "low_ready", "lr_ready", "sc_ready", "sc_out",
                   "tops", "junked", "node_in", "newtop", "st_done", "drop_ready", "fade_ready", "at_edges",
                   "t1", "t_ready", "p_ready", "p_in", "val_ready", "agg_done", "faded_ok", "acc_done", "begun") as \
                (idx_ready, in0, in1, in2, in3, w_in, att_set, att_cols, att_ready, hot_ready,
                 hott_ready, hott_out, pen_ready, mine_ready, sum_e, low_ready, lr_ready, sc_ready, sc_out,
                 tops, junked, node_in, newtop, st_done, drop_ready, fade_ready, at_edges,
                 t1, t_ready, p_ready, p_in, val_ready, agg_done, faded_ok, acc_done, begun):
            rows_in = (in0, in1, in2, in3)
            with nc.Block() as block:
                @block.gpsimd
                def _(g):
                    gather_rows(g, table, rows, idxb, idx_ready, rows_in, agg_done, begun)

                @block.sync
                def _(sp):
                    with nc.allow_non_contiguous_dma("one column"):
                        sp.dma_start(attc[:, :], att.rearrange("h (f a) -> (h f) a", a=1)).then_inc(w_in, 16)

                @block.vector
                def _(ve):
                    ve.memset(att4[:, :], 0.0).then_inc(att_set, 1)
                    ve.wait_ge(att_set, 1)
                    ve.wait_ge(w_in, 16)
                    for h in range(HEADS):
                        ins = ve.tensor_copy(att4[h * HD:(h + 1) * HD, h:h + 1], attc[h * HD:(h + 1) * HD, :])
                    ins.then_inc(att_cols, 1)
                    ve.wait_ge(att_cols, 1)
                    ve.tensor_copy(attr[:, :, :], att4[:, :].unsqueeze(2).to_broadcast([D, HEADS, BN])).then_inc(att_ready, 1)

                    def step(back, front):
                        if back:
                            i, r, b = back
                            g, k = RING * i + r, r % 2
                            ve.wait_ge(sc_out, g + 1)
                            ve.wait_ge(at_edges, g + 1)
                            ve.tensor_tensor(t[:, :], sc[k][:, :], ps_node[:, 0:TG * HEADS], ALU.subtract).then_inc(t1, 1)
                            ve.wait_ge(t1, g + 1)
                            ve.tensor_scalar(t[:, :], t[:, :], 0.0, None, ALU.min).then_inc(t_ready, 1)
                        if front:
                            fi, fr, fb = front
                            fg, fk = RING * fi + fr, fr % 2
                            one_hot(ve, c, hot[fk], fg).then_inc(hot_ready, 1)
                        if back:
                            ve.wait_ge(rows_in[r], (i + 1) * (16 * TG))
                            ve.wait_ge(p_ready, g + 1)
                            ve.tensor_tensor(val[k][:, :, 0:HD],
                                             rows[r][:, :, :].rearrange("p q (h f) -> p (q h) f", h=HEADS),
                                             p[:, :].unsqueeze(2).to_broadcast([P, TG * HEADS, HD]), ALU.mult).then_inc(p_in, 1)
                            ve.tensor_copy(val[k][:, :, HD], p[:, :]).then_inc(val_ready, 1)
                            ve.wait_ge(fade_ready, g + 1)
                            wait(ve, acc_done, g)
                            ve.tensor_tensor(faded[:, :, :], c.acc[:, bass.ds(b, 1), 0:HEADS * HW]
                                             .rearrange("p a (h f) -> p (a h) f", h=HEADS),
                                             fade[k][:, :].unsqueeze(2).to_broadcast([BN, HEADS, HW]), ALU.mult) \
                                .then_inc(faded_ok, 1)
                        if front:
                            ve.wait_ge(low_ready, fg + 1)
                            wait(ve, tops, HEADS * fg - HEADS)
                            ve.tensor_tensor(lr[fk][:, :], low[fk][:, :], ps_e[:, :], ALU.max).then_inc(lr_ready, 1)
                            ve.wait_ge(pen_ready, fg + 1)
                            wait(ve, newtop, fg)
                            for h in range(HEADS):
                                ve.wait_ge(tops, HEADS * fg + (h + 1))
                                wait(ve, junked, HEADS * fg + h)
                                ve.sem_inc(begun, 1)
                                ve.tensor_tensor_reduce(out=junk[:, :], in0=pen[fk][:, :], in1=ps_top[h % 2][:, :],
                                                        scale=1.0, scalar=-BIG, op0=ALU.add, op1=ALU.max,
                                                        accum_out=gtop[:, h:h + 1]).then_inc(junked, 1)
                            wait(ve, st_done, fg)
                            ve.tensor_scalar(node[fk][:, 0, :], c.top[:, bass.ds(fb, 1), :], 1.0, None, ALU.mult).then_inc(node_in, 1)
                            ve.wait_ge(node_in, fg + 1)
                            ve.wait_ge(junked, HEADS * fg + HEADS)
                            ve.tensor_tensor(node[fk][:, 1, :], node[fk][:, 0, :], gtop[:, :], ALU.max).then_inc(newtop, 1)
                            ve.wait_ge(newtop, fg + 1)
                            ve.tensor_scalar(c.top[:, bass.ds(fb, 1), :], node[fk][:, 1, :], 1.0, None, ALU.mult).then_inc(st_done, 1)
                            ve.tensor_tensor(drop[fk][:, :], node[fk][:, 0, :], node[fk][:, 1, :], ALU.subtract) \
                                .then_inc(drop_ready, 1)
                        if back:
                            ve.wait_ge(agg_done, g + 1)
                            ve.wait_ge(faded_ok, g + 1)
                            ve.tensor_tensor(c.acc[:, bass.ds(b, 1), 0:HEADS * HW],
                                             faded[:, :, :].rearrange("p h f -> p (h f)").unsqueeze(1),
                                             ps_acc[:, 0:HEADS * HW].unsqueeze(1), ALU.add).then_inc(acc_done, 1)
                    pipeline(nc, ve, c, step)

                @block.scalar
                def _(act):
                    first_idx(act, c, idxb, idx_ready)

                    def step(back, front):
                        if back:
                            i, r, _ = back
                            g, k = RING * i + r, r % 2
                            act.wait_ge(t_ready, g + 1)
                            wait(act, val_ready, g)
                            act.activation(p[:, :], t[:, :], ACT.Exp).then_inc(p_ready, 1)
                            act.wait_ge(drop_ready, g + 1)
                            wait(act, faded_ok, g - 1)
                            act.activation(fade[k][:, :], drop[k][:, :], ACT.Exp).then_inc(fade_ready, 1)
                        if front:
                            i, r, b = front
                            g, k = RING * i + r, r % 2
                            wait(act, sum_e, g - 1)
                            act.activation(mine[k][:, :], c.other[:, bass.ds(b, 1), :], ACT.Copy).then_inc(mine_ready, 1)
                            act.wait_ge(hott_ready, g + 1)
                            wait(act, at_edges, g - 1)
                            act.activation(hott[k][:, :], ps_hott[0:BN, :], ACT.Copy).then_inc(hott_out, 1)
                            wait(act, junked, HEADS * g - HEADS)
                            act.activation(pen[k][:, :], ps_hott[0:BN, :], ACT.Copy, bias=-BIG, scale=BIG) \
                                .then_inc(pen_ready, 1)
                            act.wait_ge(sum_e, g + 1)
                            wait(act, lr_ready, g - 1)
                            act.activation(low[k][:, :], ps_e[:, :], ACT.Copy, scale=0.2).then_inc(low_ready, 1)
                            act.wait_ge(sc_ready, g + 1)
                            wait(act, t1, g - 1)
                            act.activation(sc[k][:, :], ps_sc[:, 0:TG * HEADS], ACT.Copy).then_inc(sc_out, 1)
                            idx_ahead(act, c, idxb, idx_ready, rows_in, front)
                    pipeline(nc, act, c, step)

                @block.tensor
                def _(pe):
                    pe.wait_ge(att_ready, 1)

                    def step(back, front):
                        if back:
                            i, r, _ = back
                            g, k = RING * i + r, r % 2
                            pe.wait_ge(newtop, g + 1)
                            pe.wait_ge(hott_out, g + 1)
                            wait(pe, t1, g)
                            for q in range(TG):
                                ins = pe.matmul(ps_node[:, q * HEADS:(q + 1) * HEADS], hott[k][:, q * P:(q + 1) * P],
                                                node[k][:, 1, :], start=True, stop=True)
                            ins.then_inc(at_edges, 1)
                        if front:
                            i, r, _ = front
                            fg, fk = RING * i + r, r % 2
                            pe.wait_ge(hot_ready, fg + 1)
                            wait(pe, pen_ready, fg)
                            for q in range(TG):
                                ins = pe.transpose(ps_hott[0:BN, q * P:(q + 1) * P], hot[fk][:, q, :], c.ident[:, :])
                            ins.then_inc(hott_ready, 1)
                        if back:
                            bi, br, _ = back
                            pe.wait_ge(val_ready, g + 1)
                            pe.wait_ge(p_in, g + 1)
                            wait(pe, acc_done, g)
                            for q in range(TG):
                                ins = pe.matmul(ps_acc[:, 0:HEADS * HW], hot[k][:, q, :],
                                                val[k][:, q * HEADS:(q + 1) * HEADS, :].rearrange("p h f -> p (h f)"),
                                                start=q == 0, stop=q == TG - 1)
                            ins.then_inc(agg_done, 1)
                        if front:
                            pe.wait_ge(hott_out, fg + 1)
                            pe.wait_ge(mine_ready, fg + 1)
                            wait(pe, lr_ready, fg)
                            pe.matmul(ps_e[:, :], mine[fk][:, :], hott[fk][:, :], start=True, stop=False)
                            pe.wait_ge(rows_in[r], (i + 1) * (16 * TG))
                            for q in range(TG):
                                ins = pe.matmul(ps_e[:, q * P:(q + 1) * P], rows[r][:, q, :], c.ident[:, :],
                                                start=False, stop=q == TG - 1)
                            ins.then_inc(sum_e, 1)
                            pe.wait_ge(lr_ready, fg + 1)
                            wait(pe, sc_out, fg)
                            for q in range(TG):
                                ins = pe.matmul(ps_sc[:, q * HEADS:(q + 1) * HEADS], lr[fk][:, q * P:(q + 1) * P],
                                                att4[:, :], start=True, stop=True)
                            ins.then_inc(sc_ready, 1)
                            for h in range(HEADS):
                                wait(pe, junked, HEADS * fg + (h - 1))
                                pe.matmul(ps_top[h % 2][:, :], attr[:, h, :], lr[fk][:, :],
                                          start=True, stop=True).then_inc(tops, 1)
                    pipeline(nc, pe, None, step)


def gcn_pass(nc, c, table):
    with ExitStack() as ctx:
        sb, pb = buffers(nc, ctx)
        rows = [sb(f"rows{r}", [P, TG, D]) for r in range(RING)]
        idxb = [sb(f"idxb{r}", [P, TG], I32) for r in range(RING)]
        hot = [sb(f"hot{k}", [P, TG, BN]) for k in range(2)]
        ps_acc = [pb(f"ps_acc{k}", [BN, 512]) for k in range(2)]
        with phase(nc, "idx_ready", "in0", "in1", "in2", "in3", "hot_ready", "agg_done", "acc_done", "begun") as \
                (idx_ready, in0, in1, in2, in3, hot_ready, agg_done, acc_done, begun):
            rows_in = (in0, in1, in2, in3)
            with nc.Block() as block:
                @block.gpsimd
                def _(g):
                    gather_rows(g, table, rows, idxb, idx_ready, rows_in, agg_done, begun)

                @block.scalar
                def _(act):
                    first_idx(act, c, idxb, idx_ready)

                    def step(back, front):
                        if front:
                            idx_ahead(act, c, idxb, idx_ready, rows_in, front)
                    pipeline(nc, act, None, step)

                @block.vector
                def _(ve):
                    def step(back, front):
                        if front:
                            i, r, _ = front
                            fg, fk = RING * i + r, r % 2
                            wait(ve, agg_done, fg - 1)
                            one_hot(ve, c, hot[fk], fg, lambda q: c.wgt[:, bass.ds(fg, 1), q]).then_inc(hot_ready, 1)
                        if back:
                            i, r, b = back
                            g, k = RING * i + r, r % 2
                            ve.wait_ge(agg_done, g + 1)
                            wait(ve, acc_done, g)
                            ve.tensor_tensor(c.acc[:, bass.ds(b, 1), 0:D], c.acc[:, bass.ds(b, 1), 0:D],
                                             ps_acc[k][:, 0:D].unsqueeze(1), ALU.add).then_inc(acc_done, 1)
                    pipeline(nc, ve, c, step)

                @block.tensor
                def _(pe):
                    def step(back, front):
                        if back:
                            i, r, _ = back
                            g, k = RING * i + r, r % 2
                            pe.wait_ge(rows_in[r], (i + 1) * (16 * TG))
                            pe.wait_ge(hot_ready, g + 1)
                            wait(pe, acc_done, g - 1)
                            for q in range(TG):
                                ins = pe.matmul(ps_acc[k][:, 0:D], hot[k][:, q, :], rows[r][:, q, :],
                                                start=q == 0, stop=q == TG - 1)
                            ins.then_inc(agg_done, 1)
                    pipeline(nc, pe, None, step)


def vector_steps(nc, build):
    with phase(nc, "v") as (v,):
        with nc.Block() as block:
            @block.vector
            def _(ve):
                build(ve, chained(ve, v))


def gnn_kernel(nc, a, out):
    c = Chip()
    dram = lambda name, rows, cols: nc.dram_tensor(name, (rows, cols), F32, kind="Internal").ap()
    recs = dram("records", SLOTS, REC)
    gat_tab = dram("gat_table", N, GW)
    src_tab = dram("source_table", N, D)
    nodes = lambda ap: ap.rearrange("(b p) f -> p b f", p=BN)
    full = [BN, NB, D]
    with ExitStack() as ctx:
        sb, pb = buffers(nc, ctx)
        c.x = sb("x", full)
        c.h = sb("h", full)
        c.idx = sb("idx", [P, NG + RING, TG], I32)
        c.dlo = sb("dlo", [P, NG, TG])
        c.wgt = sb("wgt", [P, NG, TG])
        c.gblk = sb("gblk", [1, NG], I32)
        c.iota = sb("iota", [P, BN])
        c.ident = sb("ident", [P, P])
        c.ones = sb("ones_pp", [P, P])
        c.acc = sb("acc", [BN, NB, GW])
        c.st = sb("st", [BN, NB, 2])
        c.deg = sb("deg", [BN, NB])
        c.other = sb("other", full)

        sort_edges(nc, c, a["src"], a["dst"], a["edge_weight"], a["edge_attr_64"], recs)
        load_meta(nc, c, recs)
        load_rows(nc, [(c.x[:, :, :], nodes(a["x"]))])

        normalise(nc, c, c.x, c.h)
        with ExitStack() as layer:
            c.rows = buffers(nc, layer)[0]("rows", [BN, NB, GW])
            for l in range(3):
                gat_tables(nc, c, c.h, a["L0_gnn_W"][l], a["L0_gnn_a_src"][l], a["L0_gnn_a_dst"][l], gat_tab)
                gat_pass(nc, c, gat_tab)
                gat_norm(nc, c, a["L0_gnn_b"][l], c.h, add_to=c.x if l == 2 else None)

        normalise(nc, c, c.x, c.h)
        with ExitStack() as layer:
            lb = buffers(nc, layer)[0]
            w = lb("w", [D, 7, D])
            brow = lb("brow", [BN, 3, D])
            rows2 = lb("rows2", [BN, NB, 2 * D])
            agg = lb("agg", full)
            add = lb("add", full)
            cnt = lb("cnt", [BN, 2, NB])
            load_rows(nc, [(w[:, 0, :], a["L1_gnn_mW1"][0:D, :]), (w[:, 1, :], a["L1_gnn_mW1"][D:2 * D, :]),
                           (w[:, 2, :], a["L1_gnn_mW3"]), (w[:, 3, :], a["L1_gnn_uW1"][0:D, :]),
                           (w[:, 4, :], a["L1_gnn_uW1"][D:2 * D, :]), (w[:, 5, :], a["L1_gnn_uW2"]),
                           (brow[:, 0, :], a["L1_gnn_mb3"].partition_broadcast(BN)),
                           (brow[:, 1, :], a["L1_gnn_ub1"].partition_broadcast(BN)),
                           (brow[:, 2, :], a["L1_gnn_ub2"].partition_broadcast(BN))])
            linear(nc, c, [(c.h, w[:, 0:2, :].rearrange("p a f -> p (a f)"))], 2 * D, rows2, table=src_tab, table_cols=D)

            def before(ve, step):
                step(ve.tensor_copy(c.other[:, :, :], rows2[:, :, D:2 * D]))
                step(ve.memset(c.acc[:, :, :], 0.0))
            vector_steps(nc, before)
            mlp_pass(nc, c, src_tab, recs, a["L1_gnn_mW1"], a["L1_gnn_mb1"], a["L1_gnn_mW2"], a["L1_gnn_mb2"])

            def mean(ve, step):
                step(ve.tensor_copy(c.deg[:, :], c.acc[:, :, D + 1]))
                step(ve.tensor_scalar(cnt[:, 0, :], c.acc[:, :, D], 1e-8, None, ALU.add))
                step(ve.reciprocal(cnt[:, 0, :], cnt[:, 0, :]))
                step(ve.tensor_tensor(cnt[:, 1, :], c.acc[:, :, D], cnt[:, 0, :], ALU.mult))
                step(ve.tensor_tensor(agg[:, :, :], c.acc[:, :, 0:D], cnt[:, 0, :].unsqueeze(2).to_broadcast(full), ALU.mult))
                step(ve.tensor_copy(add[:, :, :], brow[:, 0:1, :].to_broadcast(full)))
                step(ve.tensor_tensor(add[:, :, :], add[:, :, :], cnt[:, 1, :].unsqueeze(2).to_broadcast(full), ALU.mult))
            vector_steps(nc, mean)
            linear(nc, c, [(agg, w[:, 2, :])], D, c.other, addend=lambda b: add[:, b, :])
            linear(nc, c, [(c.h, w[:, 3, :]), (c.other, w[:, 4, :])], D, agg, addend=lambda b: brow[:, 1, :],
                   func=ACT.Gelu_apprx_tanh)

            def residual(ve, step):
                step(ve.tensor_tensor(add[:, :, :], c.h[:, :, :], brow[:, 2:3, :].to_broadcast(full), ALU.add))
            vector_steps(nc, residual)
            linear(nc, c, [(agg, w[:, 5, :])], D, c.other, addend=lambda b: add[:, b, :])
        normalise(nc, c, c.other, None, relu=False, scale=a["L1_gnn_gamma"], shift=a["L1_gnn_beta"], add_to=c.x)

        normalise(nc, c, c.x, c.h)
        with ExitStack() as layer:
            lb = buffers(nc, layer)[0]
            w = lb("w", [D, 2 * D])
            brow = lb("brow", [BN, 2, D])
            rows2 = lb("rows2", [BN, NB, 2 * D])
            bias = lb("bias", [BN, 1, D])
            den = lb("den", [BN, NB, HEADS])
            c.top = lb("top", [BN, NB, HEADS])
            for l in ("0", "1"):
                load_rows(nc, [(w[:, 0:D], a["L2_gnn_Wl" + l]), (w[:, D:2 * D], a["L2_gnn_Wr" + l]),
                               (brow[:, 0, :], a["L2_gnn_bl" + l].partition_broadcast(BN)),
                               (brow[:, 1, :], a["L2_gnn_br" + l].partition_broadcast(BN)),
                               (bias[:, 0, :], a["L2_gnn_bias" + l].partition_broadcast(BN))])
                linear(nc, c, [(c.h, w[:, :])], 2 * D, rows2, addend=lambda b: brow[:, :, :].rearrange("p a f -> p (a f)"),
                       table=src_tab, table_cols=D)

                def before(ve, step):
                    step(ve.tensor_copy(c.other[:, :, :], rows2[:, :, D:2 * D]))
                    step(ve.memset(c.acc[:, :, :], 0.0))
                    step(ve.memset(c.top[:, :, :], -BIG))
                vector_steps(nc, before)
                gatv2_pass(nc, c, src_tab, a["L2_gnn_att" + l])

                def divide(ve, step):
                    heads = c.acc[:, :, 0:HEADS * HW].rearrange("p b (h f) -> p b h f", h=HEADS)
                    step(ve.tensor_scalar(den[:, :, :], heads[:, :, :, HD], 1e-16, None, ALU.add))
                    step(ve.reciprocal(den[:, :, :], den[:, :, :]))
                    for h in range(HEADS):
                        step(ve.tensor_tensor(c.other[:, :, h * HD:(h + 1) * HD], c.acc[:, :, h * HW:h * HW + HD],
                                              den[:, :, h:h + 1].to_broadcast([BN, NB, HD]), ALU.mult))
                    step(ve.tensor_tensor(c.other[:, :, :], c.other[:, :, :], bias[:, :, :].to_broadcast(full), ALU.add))
                vector_steps(nc, divide)
                normalise(nc, c, c.other, c.h, relu=False, scale=a["L2_gnn_g" + l], shift=a["L2_gnn_b" + l], elu=True,
                          add_to=c.x if l == "1" else None)

        normalise(nc, c, c.x, c.h)
        with ExitStack() as layer:
            lb = buffers(nc, layer)[0]
            w = lb("w", [D, 2, D])
            bias = lb("bias", [BN, 2, D])
            dinv = lb("dinv", [BN, NB])
            has = lb("has", [BN, NB])
            load_rows(nc, [(w[:, 0, :], a["L3_gnn_W1"]), (w[:, 1, :], a["L3_gnn_W2"]),
                           (bias[:, 0, :], a["L3_gnn_b1"].partition_broadcast(BN)),
                           (bias[:, 1, :], a["L3_gnn_b2"].partition_broadcast(BN))])
            with phase(nc, "v", "deg_ready", "root_ready") as (v, deg_ready, root_ready):
                with nc.Block() as block:
                    @block.vector
                    def _(ve):
                        step = chained(ve, v)
                        step(ve.tensor_scalar(has[:, :], c.deg[:, :], 0.0, None, ALU.is_gt))
                        ve.tensor_scalar(dinv[:, :], c.deg[:, :], 1e-12, None, ALU.max).then_inc(deg_ready, 1)
                        ve.wait_ge(root_ready, 1)
                        step(ve.reciprocal(dinv[:, :], dinv[:, :]))
                        step(ve.tensor_tensor(dinv[:, :], dinv[:, :], has[:, :], ALU.mult))

                    @block.scalar
                    def _(act):
                        act.wait_ge(deg_ready, 1)
                        act.activation(dinv[:, :], dinv[:, :], ACT.Sqrt).then_inc(root_ready, 1)
            for l in range(2):
                linear(nc, c, [(c.h, w[:, l, :])], D, c.other, row_scale=lambda b: dinv[:, b:b + 1],
                       table=src_tab, table_cols=D)
                vector_steps(nc, lambda ve, step: step(ve.memset(c.acc[:, :, :], 0.0)))
                gcn_pass(nc, c, src_tab)

                def after(ve, step):
                    step(ve.tensor_tensor(c.other[:, :, :], c.acc[:, :, 0:D], dinv[:, :].unsqueeze(2).to_broadcast(full), ALU.mult))
                    step(ve.tensor_tensor(c.other[:, :, :], c.other[:, :, :], bias[:, l:l + 1, :].to_broadcast(full), ALU.add))
                vector_steps(nc, after)
                n = str(l + 1)
                normalise(nc, c, c.other, c.h, scale=a["L3_gnn_g" + n], shift=a["L3_gnn_be" + n],
                          add_to=c.x if l == 1 else None)

        with phase(nc, "stored") as (stored,):
            with nc.Block() as block:
                @block.sync
                def _(sp):
                    sp.dma_start(nodes(out), c.x[:, :, :]).then_inc(stored, 16)
                    sp.wait_ge(stored, 16)


def kernel(**inputs):
    import numpy as _np
    import concourse.bacc as _bacc
    from concourse import mybir as _mybir
    from concourse.bass_utils import run_bass_kernel_spmd as _run

    nc = _bacc.Bacc("TRN2", target_bir_lowering=False, num_devices=1)
    arrays, args = {}, {}
    for name, value in inputs.items():
        a = _np.ascontiguousarray(value)
        arrays[f"in_{name}_dram"] = a
        args[name] = nc.dram_tensor(f"in_{name}_dram", a.shape, _mybir.dt.from_np(a.dtype), kind="ExternalInput").ap()
    out = nc.dram_tensor("out_0_dram", (N, D), _mybir.dt.float32, kind="ExternalOutput").ap()
    gnn_kernel(nc, args, out)
    r = _run(nc, [arrays], core_ids=[0])
    return r.results[0]["out_0_dram"]
```

```python
import concourse.bass as bass
from concourse import mybir
from contextlib import ExitStack, contextmanager

F32 = mybir.dt.float32
I32 = mybir.dt.int32
BF16 = mybir.dt.bfloat16
ALU = mybir.AluOpType
ACT = mybir.ActivationFunctionType
AX = mybir.AxisListType

N = 3125
E = 100000
D = 128
P = 128
BN = 125
NB = N // BN
TG = 4
GE = TG * P
NG = (E + NB * (GE - 1)) // GE
SLOTS = NG * GE
EP = 125
EC = E // EP
EF = 64
META = 4
REC = EF + META
SC_T = 8
LD_G = 11
RING = 8
HEADS = 4
HD = D // HEADS
EPS = 1e-5
BIG = float(2 ** 100)


class Chip:
    pass


@contextmanager
def phase(nc, *names):
    sems = [nc.alloc_semaphore(name=f"{n}_{nc.next_id()}") for n in names]
    yield sems
    nc.clear_and_free_semaphores(sems)
    nc.all_engine_barrier()


def buffers(nc, ctx):
    def sb(name, shape, dt=F32):
        return ctx.enter_context(nc.sbuf_tensor(f"{name}_{nc.next_id()}", shape, dt))

    def pb(name, shape, dt=F32):
        return ctx.enter_context(nc.psum_tensor(f"{name}_{nc.next_id()}", shape, dt))
    return sb, pb


def chained(eng, sem):
    count = [0]

    def step(ins):
        count[0] += 1
        ins.then_inc(sem, 1)
        eng.wait_ge(sem, count[0])
        return count[0]
    return step


def wait(eng, sem, value):
    if not isinstance(value, int) or value > 0:
        eng.wait_ge(sem, value)


def group_at(i, r):
    return i + r // RING, r % RING


def pipeline(nc, eng, c, depth, step):
    def blocks(g, n):
        if c is None:
            return [None] * n
        _, values = nc.values_load_multi_w_load_instructions(
            c.gblk[0:1, bass.ds(g, n)], engines=[eng.engine], min_val=0, max_val=NB - 1,
            skip_runtime_bounds_check_because="the sort counts the blocks that end before a group, NB - 1 at most")
        return values

    def plain(s, b, at):
        return [(*divmod(s + d, RING), b[s + d - at]) if 0 <= s + d < NG else None for d in range(depth)]

    b = blocks(0, depth)
    for s in range(1 - depth, 1):
        step(plain(s, b, 0))
    turns = (NG - depth) // RING
    with eng.Fori(0, turns) as i:
        b = blocks(RING * i + 1, RING + depth - 1)
        for j in range(1, RING + 1):
            step([(*group_at(i, j + d), b[j - 1 + d]) for d in range(depth)])
    last = RING * turns + 1
    b = blocks(last, NG - last)
    for s in range(last, NG):
        step(plain(s, b, last))


def sort_edges(nc, c, src, dst, w, ea, recs):
    with ExitStack() as ctx:
        sb, pb = buffers(nc, ctx)
        FR = SLOTS // P // 8
        blank = sb("blank", [P, FR, REC])
        dst_i = sb("dst_i", [EP, EC], I32)
        src_i = sb("src_i", [EP, EC], I32)
        w_f = sb("w_f", [EP, EC])
        dst_f = sb("dst_f", [EP, EC])
        blk = sb("blk", [EP, EC])
        off = sb("off_by", [EP, EC])
        oh = sb("oh", [EP, EC])
        ones = sb("ones", [EP, EC])
        scan = sb("scan", [EP, EC])
        rank = sb("rank", [EP, EC])
        tmp_i = sb("tmp_i", [EP, EC], I32)
        pos = sb("pos", [EP, EC], I32)
        meta = sb("meta", [EP, EC, META])
        bid = sb("bid", [EP, NB])
        upper = sb("upper", [EP, EP])
        tot = sb("tot", [EP, NB])
        cnt = sb("cnt", [EP, NB])
        fl = sb("fl", [EP, NB])
        fl_i = sb("fl_i", [EP, NB], I32)
        gt = sb("gt", [EP, NB])
        gend = sb("gend", [EP, NB])
        base = sb("base", [EP, NB])
        gid = sb("gid", [1, NG])
        gsum = sb("gsum", [1, NG])
        recb = [sb(f"recb{k}", [EP, SC_T, REC]) for k in range(2)]
        idxb = [sb(f"idxb{k}", [EP, SC_T], I32) for k in range(2)]
        ps = pb("ps_cnt", [EP, 2, NB])

        with phase(nc, "edges_in", "blanked", "blank_set", "consts", "v", "bin_hot", "bin_tot", "bin_scan",
                   "bin_rank", "tot_ready", "cnt_ready", "pos_ready", "ea_in0", "ea_in1", "meta_in",
                   "idx_in", "scattered0", "scattered1", "begun") as \
                (edges_in, blanked, blank_set, consts, v, bin_hot, bin_tot, bin_scan, bin_rank, tot_ready,
                 cnt_ready, pos_ready, ea_in0, ea_in1, meta_in, idx_in, scattered0, scattered1, begun):
            ea_in, scattered = (ea_in0, ea_in1), (scattered0, scattered1)
            with nc.Block() as block:
                @block.sync
                def _(sp):
                    sp.dma_start(dst_i[:, :], dst.rearrange("(p t) -> p t", p=EP)).then_inc(edges_in, 16)
                    sp.dma_start(src_i[:, :], src.rearrange("(p t) -> p t", p=EP)).then_inc(edges_in, 16)
                    sp.dma_start(w_f[:, :], w.rearrange("(p t) -> p t", p=EP)).then_inc(edges_in, 16)
                    ea_v = ea.rearrange("(p t) f -> p t f", p=EP)
                    sp.wait_ge(blank_set, 2)
                    for k in range(8):
                        rows = P * FR
                        sp.dma_start(recs[k * rows:(k + 1) * rows, :].rearrange("(p a) f -> p a f", p=P),
                                     blank[:, :, :]).then_inc(blanked, 16)
                    with sp.Fori(0, EC // SC_T // 2) as i:
                        for k in range(2):
                            sp.wait_ge(scattered[k], i * (16 * SC_T))
                            sp.dma_start(recb[k][:, :, 0:EF], ea_v[:, bass.ds((2 * i + k) * SC_T, SC_T), :]) \
                                .then_inc(ea_in[k], 16)

                @block.gpsimd
                def _(g):
                    g.memset(blank[:, :, :], 0.0).then_inc(blank_set, 1)
                    g.wait_ge(blank_set, 1)
                    g.memset(blank[:, :, EF + 1:EF + 2], -1.0).then_inc(blank_set, 1)
                    g.memset(upper[:, :], 1.0).then_inc(consts, 1)
                    g.memset(ones[:, :], 1.0).then_inc(consts, 1)
                    g.iota(bid[:, :], [[1, NB]], base=0, channel_multiplier=0,
                           allow_small_or_imprecise_dtypes=True).then_inc(consts, 1)
                    g.iota(gid[:, :], [[1, NG]], base=0, channel_multiplier=0,
                           allow_small_or_imprecise_dtypes=True).then_inc(consts, 1)
                    g.wait_ge(consts, 4)
                    g.affine_select(out=upper[:, :], in_=upper[:, :], compare_op=ALU.is_gt, fill=0.0,
                                    base=0, pattern=[[1, EP]], channel_multiplier=-1).then_inc(consts, 1)
                    g.wait_ge(blanked, 16 * 8)
                    with g.Fori(0, EC // SC_T // 2) as i:
                        for k in range(2):
                            g.wait_ge(ea_in[k], (i + 1) * 16)
                            g.wait_ge(meta_in, 2 * i + k + 1)
                            g.wait_ge(idx_in, 2 * i + k + 1)
                            g.sem_inc(begun, 1)
                            for t in range(SC_T):
                                g.indirect_dma_start(
                                    out=recs[:, :], out_offset=bass.IndirectOffsetOnAxis(ap=idxb[k][:, t:t + 1], axis=0),
                                    in_=recb[k][:, t, :], in_offset=None).then_inc(scattered[k], 16)
                    for k in range(2):
                        g.wait_ge(scattered[k], (EC // SC_T // 2) * 16 * SC_T)

                @block.tensor
                def _(pe):
                    pe.wait_ge(consts, 5)
                    pe.wait_ge(tot_ready, 1)
                    pe.matmul(ps[:, 0, :], upper[:, :], tot[:, :], start=True, stop=True)
                    pe.matmul(ps[:, 1, :], ones[:, 0:EP], tot[:, :], start=True, stop=True).then_inc(cnt_ready, 1)

                @block.vector
                def _(ve):
                    step = chained(ve, v)
                    ve.wait_ge(edges_in, 48)
                    step(ve.tensor_copy(dst_f[:, :], dst_i[:, :]))
                    step(ve.tensor_scalar(blk[:, :], dst_f[:, :], 1.0 / BN, None, ALU.mult))
                    step(ve.tensor_copy(tmp_i[:, :], blk[:, :]))
                    step(ve.tensor_copy(blk[:, :], tmp_i[:, :]))
                    step(ve.scalar_tensor_tensor(off[:, :], blk[:, :], -float(BN), dst_f[:, :], ALU.mult, ALU.add))
                    step(ve.scalar_tensor_tensor(blk[:, :], off[:, :], 0.0, blk[:, :], ALU.is_lt, ALU.subtract))
                    step(ve.tensor_scalar(blk[:, :], blk[:, :], -1.0, None, ALU.mult))
                    step(ve.scalar_tensor_tensor(off[:, :], blk[:, :], -float(BN), dst_f[:, :], ALU.mult, ALU.add))
                    step(ve.scalar_tensor_tensor(blk[:, :], off[:, :], float(BN), blk[:, :], ALU.is_ge, ALU.add))
                    step(ve.scalar_tensor_tensor(meta[:, :, 1], blk[:, :], -float(BN), dst_f[:, :], ALU.mult, ALU.add))
                    step(ve.tensor_copy(meta[:, :, 0], src_i[:, :]))
                    step(ve.tensor_copy(meta[:, :, 2], w_f[:, :]))
                    step(ve.memset(meta[:, :, 3], 0.0))
                    ve.wait_ge(consts, 5)
                    with ve.Fori(0, NB) as b:
                        ve.wait_ge(bin_tot, b)
                        ve.tensor_scalar(oh[:, :], blk[:, :], bid[:, bass.ds(b, 1)], None, ALU.is_equal) \
                            .then_inc(bin_hot, 1)
                        ve.wait_ge(bin_hot, b + 1)
                        ve.tensor_reduce(tot[:, bass.ds(b, 1)], oh[:, :], AX.X, ALU.add).then_inc(bin_tot, 1)
                    ve.wait_ge(bin_tot, NB)
                    ve.memset(gsum[:, :], 0.0).then_inc(tot_ready, 1)
                    ve.wait_ge(tot_ready, 1)
                    ve.wait_ge(cnt_ready, 1)
                    step(ve.tensor_scalar(cnt[:, :], ps[:, 1, :], float(GE - 1), 1.0 / GE, ALU.add, ALU.mult))
                    step(ve.tensor_copy(fl_i[:, :], cnt[:, :]))
                    step(ve.tensor_copy(fl[:, :], fl_i[:, :]))
                    step(ve.tensor_tensor(gt[:, :], fl[:, :], cnt[:, :], ALU.is_gt))
                    step(ve.tensor_tensor(fl[:, :], fl[:, :], gt[:, :], ALU.subtract))
                    step(ve.tensor_tensor_scan(gend[:, :], ones[:, 0:NB], fl[:, :], 0.0, ALU.mult, ALU.add))
                    step(ve.tensor_tensor(base[:, :], gend[:, :], fl[:, :], ALU.subtract))
                    step(ve.scalar_tensor_tensor(base[:, :], base[:, :], float(GE), ps[:, 0, :], ALU.mult, ALU.add))
                    with ve.Fori(0, NB) as b:
                        ve.wait_ge(bin_rank, b)
                        ve.tensor_scalar(oh[:, :], blk[:, :], bid[:, bass.ds(b, 1)], None, ALU.is_equal) \
                            .then_inc(bin_hot, 1)
                        ve.wait_ge(bin_hot, b + (NB + 1))
                        ve.tensor_tensor_scan(scan[:, :], ones[:, :], oh[:, :], base[:, bass.ds(b, 1)],
                                              ALU.mult, ALU.add).then_inc(bin_scan, 1)
                        ve.wait_ge(bin_scan, b + 1)
                        ve.sem_inc(begun, 1)
                        ve.copy_predicated(rank[:, :], oh[:, :].bitcast(I32), scan[:, :]).then_inc(bin_rank, 1)
                    ve.wait_ge(bin_rank, NB)
                    ve.tensor_scalar(pos[:, :], rank[:, :], -1.0, None, ALU.add).then_inc(pos_ready, 1)
                    for b in range(NB - 1):
                        step(ve.scalar_tensor_tensor(gsum[:, :], gid[:, :], gend[0:1, b:b + 1], gsum[:, :],
                                                     ALU.is_ge, ALU.add))
                    step(ve.tensor_copy(c.gblk[:, :], gsum[:, :]))

                @block.scalar
                def _(act):
                    act.wait_ge(pos_ready, 1)
                    with act.Fori(0, EC // SC_T // 2) as i:
                        for k in range(2):
                            act.wait_ge(scattered[k], i * (16 * SC_T))
                            act.activation(recb[k][:, :, EF:REC], meta[:, bass.ds((2 * i + k) * SC_T, SC_T), :],
                                           ACT.Copy).then_inc(meta_in, 1)
                            act.activation(idxb[k][:, :], pos[:, bass.ds((2 * i + k) * SC_T, SC_T)],
                                           ACT.Copy).then_inc(idx_in, 1)


def load_meta(nc, c, recs):
    with ExitStack() as ctx:
        sb, pb = buffers(nc, ctx)
        rb = [sb(f"rb{k}", [P, LD_G, TG, REC]) for k in range(2)]
        rv = recs.rearrange("(g p k) f -> p g (k f)", p=P, k=TG)
        with phase(nc, "rows_in0", "rows_in1", "src_out", "dst_out", "w_out", "consts") as \
                (in0, in1, src_out, dst_out, w_out, consts):
            rows_in = (in0, in1)
            with nc.Block() as block:
                @block.sync
                def _(sp):
                    with sp.Fori(0, NG // LD_G // 2) as i:
                        for k in range(2):
                            if k == 0:
                                sp.wait_ge(src_out, 2 * i)
                                sp.wait_ge(dst_out, 2 * i)
                                sp.wait_ge(w_out, 2 * i)
                            sp.dma_start(rb[k][:, :, :, :].rearrange("p g k f -> p g (k f)"),
                                         rv[:, bass.ds((2 * i + k) * LD_G, LD_G), :]).then_inc(rows_in[k], 16)

                @block.scalar
                def _(act):
                    with act.Fori(0, NG // LD_G // 2) as i:
                        for k in range(2):
                            act.wait_ge(rows_in[k], (i + 1) * 16)
                            act.activation(c.idx[:, bass.ds((2 * i + k) * LD_G, LD_G), :], rb[k][:, :, :, EF],
                                           ACT.Copy).then_inc(src_out, 1)

                @block.vector
                def _(ve):
                    ve.memset(c.idx[:, NG:NG + RING, :], 0)
                    with ve.Fori(0, NG // LD_G // 2) as i:
                        for k in range(2):
                            ve.wait_ge(rows_in[k], (i + 1) * 16)
                            ve.tensor_copy(c.dlo[:, bass.ds((2 * i + k) * LD_G, LD_G), :], rb[k][:, :, :, EF + 1]) \
                                .then_inc(dst_out, 1)
                            ve.tensor_copy(c.dlob[:, bass.ds((2 * i + k) * LD_G, LD_G), :], rb[k][:, :, :, EF + 1])
                            ve.tensor_copy(c.wgt[:, bass.ds((2 * i + k) * LD_G, LD_G), :], rb[k][:, :, :, EF + 2]) \
                                .then_inc(w_out, 1)

                @block.gpsimd
                def _(g):
                    g.iota(c.iota[:, :], [[1, BN]], base=0, channel_multiplier=0,
                           allow_small_or_imprecise_dtypes=True)
                    g.iota(c.minus_p[:, :], [[0, 1]], base=0, channel_multiplier=-1,
                           allow_small_or_imprecise_dtypes=True)
                    g.memset(c.ones[:, :], 1.0).then_inc(consts, 1)
                    g.memset(c.ident[:, :], 0.0).then_inc(consts, 1)
                    g.wait_ge(consts, 2)
                    g.affine_select(out=c.ident[:, :], in_=c.ident[:, :], compare_op=ALU.not_equal, fill=1.0,
                                    base=0, pattern=[[-1, P]], channel_multiplier=1).then_inc(consts, 1)
                    g.wait_ge(consts, 3)
                    g.tensor_copy(c.identb[:, :], c.ident[:, :])


def normalise(nc, c, x, out, relu=True, scale=None, shift=None, add_to=None, elu=False):
    with ExitStack() as ctx:
        sb, pb = buffers(nc, ctx)
        stats = sb("ln_stats", [BN, NB, 6])
        mv = sb("ln_mv", [BN, NB, 2])
        rstd = sb("ln_rstd", [BN, NB])
        eps = sb("ln_eps", [BN, 1])
        shiftm = sb("ln_shiftm", [BN, NB])
        tmp = sb("ln_tmp", [BN, NB, D])
        tmp2 = sb("ln_tmp2", [BN, NB, D])
        rows = sb("ln_rows", [BN, 2, D])
        with phase(nc, "v", "rows_in", "var_ready", "std_ready", "coef_ready", "normed", "exped", "pre") as \
                (v, rows_in, var_ready, std_ready, coef_ready, normed, exped, pre):
            plain = scale is None
            fn = ACT.Relu if plain and relu else ACT.Identity
            target = out if plain and add_to is None else tmp
            with nc.Block() as block:
                @block.sync
                def _(sp):
                    if not plain:
                        sp.dma_start(rows[:, 0, :], scale.partition_broadcast(BN)).then_inc(rows_in, 16)
                        sp.dma_start(rows[:, 1, :], shift.partition_broadcast(BN)).then_inc(rows_in, 16)

                @block.scalar
                def _(act):
                    act.wait_ge(var_ready, 1)
                    act.activation(rstd[:, :], mv[:, :, 1], ACT.Sqrt, bias=eps[:, 0:1]).then_inc(std_ready, 1)
                    act.wait_ge(coef_ready, 1)
                    for b in range(NB):
                        ins = act.activation(target[:, b, :], x[:, b, :], fn, bias=shiftm[:, b:b + 1],
                                             scale=rstd[:, b:b + 1])
                    ins.then_inc(normed, 1)
                    if elu:
                        act.wait_ge(pre, 1)
                        act.activation(tmp2[:, :, :], tmp2[:, :, :], ACT.Exp).then_inc(exped, 1)

                @block.vector
                def _(ve):
                    step = chained(ve, v)
                    for b in range(NB):
                        ins = ve.bn_stats(stats[:, b, :], x[:, b, :])
                    step(ins)
                    for b in range(NB):
                        ins = ve.bn_aggr(mv[:, b, :], stats[:, b, :])
                    step(ins)
                    ve.memset(eps[:, :], EPS).then_inc(var_ready, 1)
                    ve.wait_ge(std_ready, 1)
                    step(ve.reciprocal(rstd[:, :], rstd[:, :]))
                    ve.scalar_tensor_tensor(shiftm[:, :], mv[:, :, 0], -1.0, rstd[:, :], ALU.mult, ALU.mult) \
                        .then_inc(coef_ready, 1)
                    ve.wait_ge(normed, 1)
                    if not plain:
                        ve.wait_ge(rows_in, 32)
                        step(ve.tensor_tensor(tmp[:, :, :], tmp[:, :, :],
                                              rows[:, 0:1, :].to_broadcast([BN, NB, D]), ALU.mult))
                        step(ve.tensor_tensor(tmp[:, :, :], tmp[:, :, :],
                                              rows[:, 1:2, :].to_broadcast([BN, NB, D]), ALU.add))
                    if elu:
                        ve.tensor_scalar(tmp2[:, :, :], tmp[:, :, :], 0.0, None, ALU.min).then_inc(pre, 1)
                        step(ve.tensor_scalar(tmp[:, :, :], tmp[:, :, :], 0.0, None, ALU.max))
                        ve.wait_ge(exped, 1)
                        step(ve.scalar_tensor_tensor(tmp[:, :, :], tmp2[:, :, :], -1.0, tmp[:, :, :],
                                                     ALU.add, ALU.add))
                    elif not plain and relu:
                        step(ve.tensor_scalar(tmp[:, :, :], tmp[:, :, :], 0.0, None, ALU.max))
                    if add_to is not None:
                        step(ve.tensor_tensor(add_to[:, :, :], add_to[:, :, :], tmp[:, :, :], ALU.add))
                    elif not plain:
                        step(ve.tensor_copy(out[:, :, :], tmp[:, :, :]))


def linear(nc, c, terms, width, out, addend=None, func=None, table=None, table_cols=None, row_scale=None):
    with ExitStack() as ctx:
        sb, pb = buffers(nc, ctx)
        nt = len(terms)
        xt = [[sb(f"lin_xt{t}{k}", [P, BN]) for k in range(2)] for t in range(nt)]
        pt = [pb(f"lin_pt{k}", [P, nt, 512]) for k in range(2)]
        po = [pb(f"lin_po{k}", [BN, 512]) for k in range(2)]
        with phase(nc, "turned", "turned_out", "summed", "added", "applied", "stored") as \
                (turned, turned_out, summed, added, applied, stored):
            with nc.Block() as block:
                @block.tensor
                def _(pe):
                    for s in range(NB + 1):
                        if s < NB:
                            wait(pe, turned_out, s - 1)
                            for t, (x, _) in enumerate(terms):
                                ins = pe.transpose(pt[s % 2][:, t, 0:BN], x[:, s, :], c.ident[0:BN, 0:BN])
                            ins.then_inc(turned, 1)
                        if s > 0:
                            b = s - 1
                            pe.wait_ge(turned_out, b + 1)
                            wait(pe, added, b - 1)
                            for t, (_, wt) in enumerate(terms):
                                ins = pe.matmul(po[b % 2][:, 0:width], xt[t][b % 2][:, :], wt,
                                                start=t == 0, stop=t == nt - 1)
                            ins.then_inc(summed, 1)

                @block.scalar
                def _(act):
                    for b in range(NB):
                        act.wait_ge(turned, b + 1)
                        wait(act, summed, b - 1)
                        for t in range(nt):
                            ins = act.activation(xt[t][b % 2][:, :], pt[b % 2][:, t, 0:BN], ACT.Copy)
                        ins.then_inc(turned_out, 1)
                    if func is not None:
                        act.wait_ge(added, NB)
                        for b in range(0, NB, 5):
                            ins = act.activation(out[:, b:b + 5, :], out[:, b:b + 5, :], func)
                        ins.then_inc(applied, 1)

                @block.vector
                def _(ve):
                    for b in range(NB):
                        ve.wait_ge(summed, b + 1)
                        if addend is not None:
                            ins = ve.tensor_tensor(out[:, b, 0:width], po[b % 2][:, 0:width], addend(b), ALU.add)
                        elif row_scale is not None:
                            ins = ve.tensor_scalar(out[:, b, 0:width], po[b % 2][:, 0:width], row_scale(b), None, ALU.mult)
                        else:
                            ins = ve.tensor_copy(out[:, b, 0:width], po[b % 2][:, 0:width])
                        ins.then_inc(added, 1)

                @block.sync
                def _(sp):
                    if table is not None:
                        sp.wait_ge(added, NB)
                        sp.dma_start(table.rearrange("(b p) f -> p b f", p=BN), out[:, :, 0:table_cols]) \
                            .then_inc(stored, 16)
                        sp.wait_ge(stored, 16)


def gather_rows(g, table, rows, idxb, idx_ready, rows_in, agg_done, begun):
    def gather(i, r):
        n = RING * i + r
        g.wait_ge(idx_ready, n + 1)
        wait(g, agg_done, n - RING + 1)
        g.sem_inc(begun, 1)
        for k in range(TG):
            g.indirect_dma_start(out=rows[r][:, k, :], out_offset=None, in_=table,
                                 in_offset=bass.IndirectOffsetOnAxis(ap=idxb[r][:, k:k + 1], axis=0)) \
                .then_inc(rows_in[r], 16)
    for r in range(RING):
        gather(0, r)
    with g.Fori(1, NG // RING) as i:
        for r in range(RING):
            gather(i, r)
    for r in range(NG % RING):
        gather(NG // RING, r)


def next_idx(act, c, idxb, idx_ready, rows_in, i, r):
    act.wait_ge(rows_in[r], (i + 1) * (16 * TG))
    act.activation(idxb[r][:, :], c.idx[:, bass.ds(RING * i + r + RING, 1), :], ACT.Copy).then_inc(idx_ready, 1)


def first_idx(act, c, idxb, idx_ready):
    for r in range(RING):
        act.activation(idxb[r][:, :], c.idx[:, r, :], ACT.Copy).then_inc(idx_ready, 1)


def spread_targets(pe, c, ps, g):
    for q in range(TG):
        ins = pe.matmul(ps[0:BN, q * P:(q + 1) * P], c.dlob[:, bass.ds(g, 1), q].to_broadcast([P, BN]), c.identb[:, :],
                        start=True, stop=True)
    return ins


def one_hot(ve, c, out, g, weight=None):
    if weight is None:
        return ve.tensor_tensor(out[:, :, :], c.iota[:, :].unsqueeze(1).to_broadcast([P, TG, BN]),
                                c.dlo[:, bass.ds(g, 1), :].rearrange("p a q -> p (a q)").unsqueeze(2)
                                .to_broadcast([P, TG, BN]), ALU.is_equal)
    for k in range(TG):
        ins = ve.tensor_scalar(out[:, k, :], c.iota[:, :], c.dlo[:, bass.ds(g, 1), k], weight(k), ALU.is_equal, ALU.mult)
    return ins


GA = 131
GW = 136
PART = 2 * GA
PARTS = 3


def gat_pass(nc, c, table):
    with ExitStack() as ctx:
        sb, pb = buffers(nc, ctx)
        rows = [sb(f"rows{r}", [P, TG, GW]) for r in range(RING)]
        idxb = [sb(f"idxb{r}", [P, TG], I32) for r in range(RING)]
        dist = sb("dist", [BN, GE])
        hott = [sb(f"hott{r}", [BN, GE], BF16) for r in range(RING)]
        pen = [sb(f"pen{k}", [BN, GE]) for k in range(2)]
        hotp = [sb(f"hotp{k}", [P, TG, BN]) for k in range(2)]
        parts = sb("parts", [P, TG, PARTS], BF16)
        srow = sb("srow", [TG * PARTS, P], BF16)
        sel = sb("sel", [TG * PARTS, TG, BN], BF16)
        junk = sb("junk", [BN, GE])
        top = sb("top", [BN, 1])
        node = [sb(f"node{k}", [BN, 5]) for k in range(2)]
        res = sb("res", [BN, 2])
        cuts = [sb(f"cuts{k}", [BN, PARTS, 2], BF16) for k in range(2)]
        there = sb("there", [P, TG, 2])
        fade = [sb(f"fade{k}", [BN, 1]) for k in range(2)]
        t = sb("t", [P, TG])
        p = [sb(f"p{k}", [P, TG]) for k in range(2)]
        ps_tgt = pb("ps_tgt", [P, 512])
        ps_srow = pb("ps_srow", [TG * PARTS, 1024], BF16)
        ps_s = [pb(f"ps_s{k}", [P, 512]) for k in range(2)]
        ps_node = [pb(f"ps_node{k}", [P, TG, PARTS, 2]) for k in range(2)]
        ps_acc = [pb(f"ps_acc{k}", [BN, 512]) for k in range(2)]
        with phase(nc, "idx_ready", "in0", "in1", "in2", "in3", "in4", "in5", "in6", "in7", "sel_set", "tgt_ready", "dist_ready", "hott_ready",
                   "pen_ready", "parts_in", "srow_ready", "srow_out", "s_ready", "top_done", "node_in", "tgt_in", "newtop", "st_done", "y_done",
                   "max_ready", "fade_ready", "cut1", "cut2", "cut3", "cut4", "at_edges", "summed", "t1", "t2", "t3", "t_ready", "p_ready", "hotp_ready",
                   "agg_done", "acc_done", "begun") as \
                (idx_ready, in0, in1, in2, in3, in4, in5, in6, in7, sel_set, tgt_ready, dist_ready, hott_ready,
                 pen_ready, parts_in, srow_ready, srow_out, s_ready, top_done, node_in, tgt_in, newtop, st_done, y_done,
                 max_ready, fade_ready, cut1, cut2, cut3, cut4, at_edges, summed, t1, t2, t3, t_ready, p_ready, hotp_ready,
                 agg_done, acc_done, begun):
            rows_in = (in0, in1, in2, in3, in4, in5, in6, in7)
            with nc.Block() as block:
                @block.gpsimd
                def _(g):
                    g.memset(sel[:, :, :], 1.0).then_inc(sel_set, 1)
                    g.wait_ge(sel_set, 1)
                    g.affine_select(out=sel[:, :, :], in_=sel[:, :, :], compare_op=ALU.is_ge, fill=0.0, base=0,
                                    pattern=[[-PARTS, TG], [0, BN]], channel_multiplier=1).then_inc(sel_set, 1)
                    g.wait_ge(sel_set, 2)
                    g.affine_select(out=sel[:, :, :], in_=sel[:, :, :], compare_op=ALU.is_ge, fill=0.0, base=PARTS - 1,
                                    pattern=[[PARTS, TG], [0, BN]], channel_multiplier=-1).then_inc(sel_set, 1)
                    gather_rows(g, table, rows, idxb, idx_ready, rows_in, agg_done, begun)

                @block.tensor
                def _(pe):
                    pe.wait_ge(sel_set, 3)

                    def step(stages):
                        sums, weights, _, scores, masks = stages
                        if masks:
                            g = RING * masks[0] + masks[1]
                            wait(pe, dist_ready, g)
                            spread_targets(pe, c, ps_tgt, g).then_inc(tgt_ready, 1)
                        if scores:
                            i, r, _ = scores
                            g, k = RING * i + r, r % 2
                            pe.wait_ge(parts_in, g + 1)
                            wait(pe, srow_out, g)
                            pe.sem_inc(begun, 1)
                            pe.transpose(ps_srow[:, 0:P], parts[:, :, :].rearrange("p q m -> p (q m)"),
                                         c.identb[:, :]).then_inc(srow_ready, 1)
                        if weights:
                            i, r, _ = weights
                            g, k = RING * i + r, r % 2
                            pe.wait_ge(cut4, g + 1)
                            for q in range(TG):
                                ins = pe.matmul(ps_node[k][:, q, :, :], hott[r][:, q * P:(q + 1) * P], cuts[k][:, :, :],
                                                start=True, stop=True)
                            ins.then_inc(at_edges, 1)
                        if sums:
                            i, r, _ = sums
                            g, k = RING * i + r, r % 2
                            pe.wait_ge(hotp_ready, g + 1)
                            wait(pe, acc_done, g - 1)
                            for q in range(TG):
                                ins = pe.matmul(ps_acc[k][:, 0:GA], hotp[k][:, q, :], rows[r][:, q, 0:GA],
                                                start=q == 0, stop=q == TG - 1)
                            ins.then_inc(agg_done, 1)
                        if scores:
                            i, r, _ = scores
                            g, k = RING * i + r, r % 2
                            pe.wait_ge(srow_out, g + 1)
                            wait(pe, top_done, g - 1)
                            for q in range(TG):
                                ins = pe.matmul(ps_s[k][0:BN, q * P:(q + 1) * P], sel[:, q, :], srow[:, :],
                                                start=True, stop=True)
                            ins.then_inc(s_ready, 1)
                    pipeline(nc, pe, None, 5, step)

                @block.vector
                def _(ve):
                    def step(stages):
                        sums, weights, maxima, _, _ = stages
                        if sums:
                            i, r, b = sums
                            g, k = RING * i + r, r % 2
                            ve.wait_ge(p_ready, g + 1)
                            wait(ve, agg_done, g - 1)
                            one_hot(ve, c, hotp[k], g, lambda q: p[k][:, q:q + 1]).then_inc(hotp_ready, 1)
                        if maxima:
                            mi, mr, mb = maxima
                            mg, mk = RING * mi + mr, mr % 2
                            ve.wait_ge(pen_ready, mg + 1)
                            ve.wait_ge(s_ready, mg + 1)
                            wait(ve, newtop, mg)
                            wait(ve, st_done, mg)
                            ve.tensor_scalar(node[mk][:, 0:1], c.st[:, bass.ds(mb, 1), 1], 1.0, None, ALU.mult) \
                                .then_inc(node_in, 1)
                            ve.tensor_scalar(node[mk][:, 4:5], c.st[:, bass.ds(mb, 1), 0], 1.0, None, ALU.mult) \
                                .then_inc(tgt_in, 1)
                            ve.sem_inc(begun, 1)
                            ve.tensor_tensor_reduce(out=junk[:, :], in0=pen[mk][:, :], in1=ps_s[mk][0:BN, :], scale=1.0,
                                                    scalar=-BIG, op0=ALU.add, op1=ALU.max, accum_out=top[:, :]) \
                                .then_inc(top_done, 1)
                        if weights:
                            wi, wr, _ = weights
                            wg, wk = RING * wi + wr, wr % 2
                            ve.wait_ge(rows_in[wr], (wi + 1) * (16 * TG))
                            ve.wait_ge(at_edges, wg + 1)
                            ve.tensor_reduce(there[:, :, :], ps_node[wk][:, :, :, :].rearrange("p q m v -> p q v m"),
                                             AX.X, ALU.add).then_inc(summed, 1)
                        if maxima:
                            ve.wait_ge(node_in, mg + 1)
                            ve.wait_ge(top_done, mg + 1)
                            ve.tensor_tensor(node[mk][:, 1:2], node[mk][:, 0:1], top[:, :], ALU.max).then_inc(newtop, 1)
                        if weights:
                            ve.wait_ge(summed, wg + 1)
                            wait(ve, p_ready, wg)
                            ve.tensor_tensor(t[:, :], rows[wr][:, :, D], there[:, :, 1], ALU.add).then_inc(t1, 1)
                        if maxima:
                            ve.wait_ge(newtop, mg + 1)
                            ve.wait_ge(tgt_in, mg + 1)
                            ve.tensor_scalar(node[mk][:, 2:4], node[mk][:, 0:2], node[mk][:, 4:5], None, ALU.add) \
                                .then_inc(y_done, 1)
                        if weights:
                            ve.wait_ge(t1, wg + 1)
                            ve.scalar_tensor_tensor(t[:, :], t[:, :], 0.2, t[:, :], ALU.mult, ALU.max).then_inc(t2, 1)
                        if maxima:
                            ve.wait_ge(y_done, mg + 1)
                            ve.scalar_tensor_tensor(node[mk][:, 2:4], node[mk][:, 2:4], 0.2, node[mk][:, 2:4],
                                                    ALU.mult, ALU.max).then_inc(max_ready, 1)
                        if weights:
                            ve.wait_ge(t2, wg + 1)
                            ve.tensor_tensor(t[:, :], t[:, :], there[:, :, 0], ALU.subtract).then_inc(t3, 1)
                        if maxima:
                            ve.wait_ge(max_ready, mg + 1)
                            wait(ve, at_edges, mg - 1)
                            ve.tensor_copy(cuts[mk][:, 0, :], node[mk][:, 3:5]).then_inc(cut1, 1)
                        if weights:
                            ve.wait_ge(t3, wg + 1)
                            ve.tensor_scalar(t[:, :], t[:, :], 0.0, None, ALU.min).then_inc(t_ready, 1)
                        if maxima:
                            ve.wait_ge(cut1, mg + 1)
                            ve.tensor_tensor(res[:, :], node[mk][:, 3:5], cuts[mk][:, 0, :], ALU.subtract).then_inc(cut2, 1)
                            ve.tensor_scalar(c.st[:, bass.ds(mb, 1), 1], node[mk][:, 1:2], 1.0, None, ALU.mult) \
                                .then_inc(st_done, 1)
                            ve.wait_ge(cut2, mg + 1)
                            ve.tensor_copy(cuts[mk][:, 1, :], res[:, :]).then_inc(cut3, 1)
                            ve.wait_ge(cut3, mg + 1)
                            ve.tensor_tensor(cuts[mk][:, 2, :], res[:, :], cuts[mk][:, 1, :], ALU.subtract).then_inc(cut4, 1)
                        if sums:
                            ve.wait_ge(agg_done, g + 1)
                            ve.wait_ge(fade_ready, g + 1)
                            wait(ve, acc_done, g)
                            ve.scalar_tensor_tensor(c.acc[:, bass.ds(b, 1), 0:GA], c.acc[:, bass.ds(b, 1), 0:GA],
                                                    fade[k][:, 0:1], ps_acc[k][:, 0:GA], ALU.mult, ALU.add) \
                                .then_inc(acc_done, 1)
                    pipeline(nc, ve, c, 5, step)

                @block.scalar
                def _(act):
                    first_idx(act, c, idxb, idx_ready)

                    def step(stages):
                        sums, weights, _, scores, masks = stages
                        if scores:
                            i, r, _ = scores
                            sg, sk = RING * i + r, r % 2
                            act.wait_ge(rows_in[r], (i + 1) * (16 * TG))
                            wait(act, srow_ready, sg)
                            act.activation(parts[:, :, :], rows[r][:, :, :].bitcast(BF16)[:, :, PART:PART + PARTS],
                                           ACT.Copy).then_inc(parts_in, 1)
                        if weights:
                            wi, wr, _ = weights
                            wg, wk = RING * wi + wr, wr % 2
                            act.wait_ge(max_ready, wg + 1)
                            wait(act, acc_done, wg - 1)
                            act.activation(fade[wk][:, :], node[wk][:, 3:4], ACT.Exp, bias=node[wk][:, 2:3], scale=-1.0) \
                                .then_inc(fade_ready, 1)
                        if scores:
                            act.wait_ge(srow_ready, sg + 1)
                            wait(act, s_ready, sg)
                            act.activation(srow[:, :], ps_srow[:, 0:P], ACT.Copy).then_inc(srow_out, 1)
                        if masks:
                            mi, mr, _ = masks
                            mg = RING * mi + mr
                            act.wait_ge(tgt_ready, mg + 1)
                            wait(act, hott_ready, mg)
                            act.activation(dist[:, :], ps_tgt[0:BN, :], ACT.Abs, bias=c.minus_p[0:BN, :]).then_inc(dist_ready, 1)
                        if sums:
                            next_idx(act, c, idxb, idx_ready, rows_in, sums[0], sums[1])
                        if masks:
                            act.wait_ge(dist_ready, mg + 1)
                            act.activation(hott[mr][:, :], dist[:, :], ACT.Relu, bias=c.ones[0:BN, 0:1], scale=-1.0) \
                                .then_inc(hott_ready, 1)
                        if weights:
                            act.wait_ge(t_ready, wg + 1)
                            wait(act, hotp_ready, wg - 1)
                            act.activation(p[wk][:, :], t[:, :], ACT.Exp).then_inc(p_ready, 1)
                        if scores:
                            act.wait_ge(hott_ready, sg + 1)
                            wait(act, top_done, sg - 1)
                            act.activation(pen[sk][:, :], hott[r][:, :], ACT.Copy, bias=-BIG, scale=BIG).then_inc(pen_ready, 1)
                    pipeline(nc, act, None, 5, step)


def gat_tables(nc, c, z, w, a_src, a_dst, table):
    with ExitStack() as ctx:
        sb, pb = buffers(nc, ctx)
        wx = sb("wx", [D, D + 2])
        wt = sb("wt", [D, D])
        a2 = sb("a2", [D, 2])
        pw = pb("pw", [D, D])
        pa = pb("pa", [D, 2])
        with phase(nc, "w_in", "w_turned", "w_out", "wa", "wa_out") as (w_in, w_turned, w_out, wa, wa_out):
            with nc.Block() as block:
                @block.sync
                def _(sp):
                    sp.dma_start(wx[:, 0:D], w).then_inc(w_in, 16)
                    with nc.allow_non_contiguous_dma("one column"):
                        sp.dma_start(a2[:, 0:1], a_src.rearrange("(f a) -> f a", a=1)).then_inc(w_in, 16)
                        sp.dma_start(a2[:, 1:2], a_dst.rearrange("(f a) -> f a", a=1)).then_inc(w_in, 16)

                @block.tensor
                def _(pe):
                    pe.wait_ge(w_in, 48)
                    pe.transpose(pw[:, :], wx[:, 0:D], c.ident[:, :]).then_inc(w_turned, 1)
                    pe.wait_ge(w_out, 1)
                    pe.matmul(pa[:, :], wt[:, :], a2[:, :], start=True, stop=True).then_inc(wa, 1)

                @block.vector
                def _(ve):
                    ve.memset(c.rows[:, :, 0:GW], 0.0)
                    ve.wait_ge(w_turned, 1)
                    ve.tensor_copy(wt[:, :], pw[:, :]).then_inc(w_out, 1)
                    ve.wait_ge(wa, 1)
                    ve.tensor_copy(wx[:, D:D + 2], pa[:, :]).then_inc(wa_out, 1)
                    ve.wait_ge(wa_out, 1)
                    ve.memset(c.rows[:, :, D + 2:D + 3], 1.0)
        linear(nc, c, [(z, wx[:, :])], D + 2, c.rows)
        res = sb("res", [BN, NB])
        parts = c.rows[:, :, :].bitcast(BF16)
        score = c.rows[:, :, D]
        with phase(nc, "v", "split", "stored") as (v, split, stored):
            with nc.Block() as block:
                @block.vector
                def _(ve):
                    step = chained(ve, v)
                    step(ve.tensor_copy(parts[:, :, PART], score))
                    step(ve.tensor_tensor(res[:, :], score, parts[:, :, PART], ALU.subtract))
                    step(ve.tensor_copy(parts[:, :, PART + 1], res[:, :]))
                    ve.tensor_tensor(parts[:, :, PART + 2], res[:, :], parts[:, :, PART + 1], ALU.subtract).then_inc(split, 1)
                    ve.tensor_copy(c.acc[:, :, 0:GA], c.rows[:, :, 0:GA])
                    ve.tensor_copy(c.st[:, :, 0], c.rows[:, :, D + 1])
                    ve.tensor_copy(c.st[:, :, 1], c.rows[:, :, D])

                @block.sync
                def _(sp):
                    sp.wait_ge(split, 1)
                    sp.dma_start(table.rearrange("(b p) f -> p b f", p=BN), c.rows[:, :, :]).then_inc(stored, 16)
                    sp.wait_ge(stored, 16)


def gat_norm(nc, c, bias, out, add_to=None):
    with ExitStack() as ctx:
        sb, pb = buffers(nc, ctx)
        z = sb("z", [BN, NB, D])
        sq = sb("sq", [BN, NB, D])
        rden = sb("rden", [BN, NB])
        bias_r = sb("bias_r", [BN, 1, D])
        mean = sb("mean", [BN, 1, D])
        std = sb("std", [BN, 1, D])
        eps = sb("eps", [BN, 1])
        ps = [pb(f"ps_bn{k}", [BN, D]) for k in range(2)]
        with phase(nc, "v", "b_in", "z_ready", "mean_ready", "centred", "squared", "var_ready", "std_ready") as \
                (v, b_in, z_ready, mean_ready, centred, squared, var_ready, std_ready):
            with nc.Block() as block:
                @block.sync
                def _(sp):
                    sp.dma_start(bias_r[:, 0, :], bias.partition_broadcast(BN)).then_inc(b_in, 16)

                @block.vector
                def _(ve):
                    step = chained(ve, v)
                    full = [BN, NB, D]
                    step(ve.reciprocal(rden[:, :], c.acc[:, :, D + 2]))
                    step(ve.tensor_tensor(z[:, :, :], c.acc[:, :, 0:D], rden[:, :].unsqueeze(2).to_broadcast(full), ALU.mult))
                    ve.wait_ge(b_in, 16)
                    ve.memset(eps[:, :], EPS)
                    ve.tensor_tensor(z[:, :, :], z[:, :, :], bias_r[:, :, :].to_broadcast(full), ALU.add).then_inc(z_ready, 1)
                    ve.wait_ge(mean_ready, 1)
                    step(ve.tensor_scalar(mean[:, 0, :], ps[0][:, :], 1.0 / N, None, ALU.mult))
                    ve.tensor_tensor(z[:, :, :], z[:, :, :], mean[:, :, :].to_broadcast(full), ALU.subtract).then_inc(centred, 1)
                    ve.wait_ge(std_ready, 1)
                    step(ve.reciprocal(std[:, :, :], std[:, :, :]))
                    step(ve.tensor_tensor(z[:, :, :], z[:, :, :], std[:, :, :].to_broadcast(full), ALU.mult))
                    if add_to is None:
                        step(ve.tensor_scalar(out[:, :, :], z[:, :, :], 0.0, None, ALU.max))
                    else:
                        step(ve.scalar_tensor_tensor(add_to[:, :, :], z[:, :, :], 0.0, add_to[:, :, :], ALU.max, ALU.add))

                @block.scalar
                def _(act):
                    act.wait_ge(centred, 1)
                    act.activation(sq[:, :, :], z[:, :, :], ACT.Square).then_inc(squared, 1)
                    act.wait_ge(var_ready, 1)
                    act.activation(std[:, 0, :], ps[1][:, :], ACT.Sqrt, bias=eps[:, 0:1], scale=1.0 / N).then_inc(std_ready, 1)

                @block.tensor
                def _(pe):
                    for k, (x, ready, done) in enumerate(((z, z_ready, mean_ready), (sq, squared, var_ready))):
                        pe.wait_ge(ready, 1)
                        for b in range(NB):
                            ins = pe.matmul(ps[k][:, :], c.ones[0:BN, 0:BN], x[:, b, :], start=b == 0, stop=b == NB - 1)
                        ins.then_inc(done, 1)


def load_rows(nc, pairs):
    with phase(nc, "loaded") as (loaded,):
        with nc.Block() as block:
            @block.sync
            def _(sp):
                for dst, src in pairs:
                    sp.dma_start(dst, src).then_inc(loaded, 16)
                sp.wait_ge(loaded, 16 * len(pairs))


MA = D + 2


def mlp_pass(nc, c, table, recs, w1, b1, w2, b2):
    with ExitStack() as ctx:
        sb, pb = buffers(nc, ctx)
        rows = [sb(f"rows{r}", [P, TG, D]) for r in range(RING)]
        feat = [sb(f"feat{r}", [P, TG, EF]) for r in range(RING)]
        idxb = [sb(f"idxb{r}", [P, TG], I32) for r in range(RING)]
        hot = [sb(f"hot{r}", [P, TG, BN]) for r in range(RING)]
        dist = sb("dist", [BN, GE])
        hott = [sb(f"hott{k}", [BN, GE], BF16) for k in range(2)]
        featt = [sb(f"featt{k}", [EF, GE]) for k in range(2)]
        g1 = [sb(f"g1{k}", [D, GE]) for k in range(2)]
        u2 = sb("u2", [P, TG, D])
        g2 = [sb(f"g2{k}", [P, TG, MA]) for k in range(2)]
        w1c = sb("w1c", [EF, D])
        w2s = sb("w2s", [D, D])
        b1c = sb("b1c", [D, 1])
        b2r = sb("b2r", [P, 1, D])
        ps_tgt = pb("ps_tgt", [P, 512])
        ps_featt = pb("ps_featt", [P, 512])
        ps_1 = [pb(f"ps_1{k}", [D, 512]) for k in range(2)]
        ps_2 = [pb(f"ps_2{k}", [P, TG, D]) for k in range(2)]
        ps_acc = [pb(f"ps_acc{k}", [BN, 512]) for k in range(2)]
        rv = recs.rearrange("(g p k) f -> p g k f", p=P, k=TG)
        with phase(nc, "idx_ready", "in0", "in1", "in2", "in3", "in4", "in5", "in6", "in7", "feat0", "feat1", "feat2", "feat3", "feat4", "feat5", "feat6", "feat7", "w_in", "ones_set",
                   "hot_ready", "tgt_ready", "dist_ready", "hott_ready", "featt_ready", "featt_out",
                   "sum1", "gelu1", "sum2", "biased", "wcol", "gelu2", "agg_done", "acc_done", "begun") as \
                (idx_ready, in0, in1, in2, in3, in4, in5, in6, in7, feat0, feat1, feat2, feat3, feat4, feat5, feat6, feat7, w_in, ones_set,
                 hot_ready, tgt_ready, dist_ready, hott_ready, featt_ready, featt_out,
                 sum1, gelu1, sum2, biased, wcol, gelu2, agg_done, acc_done, begun):
            rows_in, feat_in = (in0, in1, in2, in3, in4, in5, in6, in7), (feat0, feat1, feat2, feat3, feat4, feat5, feat6, feat7)
            with nc.Block() as block:
                @block.gpsimd
                def _(g):
                    gather_rows(g, table, rows, idxb, idx_ready, rows_in, agg_done, begun)

                @block.sync
                def _(sp):
                    sp.dma_start(w1c[:, :], w1[2 * D:2 * D + EF, :]).then_inc(w_in, 16)
                    sp.dma_start(w2s[:, :], w2).then_inc(w_in, 16)
                    with nc.allow_non_contiguous_dma("one column"):
                        sp.dma_start(b1c[:, :], b1.rearrange("(f a) -> f a", a=1)).then_inc(w_in, 16)
                    sp.dma_start(b2r[:, 0, :], b2.partition_broadcast(P)).then_inc(w_in, 16)

                    def load(i, r):
                        wait(sp, featt_ready, RING * i + r - RING + 1)
                        sp.dma_start(feat[r][:, :, :], rv[:, bass.ds(RING * i + r, 1), :, 0:EF] if not isinstance(i, int)
                                     else rv[:, RING * i + r, :, 0:EF]).then_inc(feat_in[r], 16)
                    for r in range(RING):
                        load(0, r)
                    with sp.Fori(1, NG // RING) as i:
                        for r in range(RING):
                            load(i, r)
                    for r in range(NG % RING):
                        load(NG // RING, r)

                @block.tensor
                def _(pe):
                    pe.wait_ge(w_in, 64)
                    pe.wait_ge(ones_set, 2)

                    def step(stages):
                        last, mid, first = stages
                        if last:
                            i, r, _ = last
                            g, k = RING * i + r, r % 2
                            pe.wait_ge(gelu1, g + 1)
                            wait(pe, biased, g - 1)
                            for q in range(TG):
                                ins = pe.matmul(ps_2[k][:, q, :], g1[k][:, q * P:(q + 1) * P], w2s[:, :],
                                                start=True, stop=True)
                            ins.then_inc(sum2, 1)
                        if mid:
                            i, r, b = mid
                            mg, mk = RING * i + r, r % 2
                            pe.wait_ge(hott_ready, mg + 1)
                            wait(pe, gelu1, mg - 1)
                            for m in range(PARTS):
                                pe.matmul(ps_1[mk][:, :], c.mine[:, bass.ds(b, 1), m, :].rearrange("p a f -> p (a f)"),
                                          hott[mk][:, :], start=m == 0, stop=False)
                            pe.wait_ge(featt_out, mg + 1)
                            pe.matmul(ps_1[mk][:, :], w1c[:, :], featt[mk][:, :], start=False, stop=False)
                            pe.wait_ge(rows_in[r], (i + 1) * (16 * TG))
                            for q in range(TG):
                                ins = pe.matmul(ps_1[mk][:, q * P:(q + 1) * P], rows[r][:, q, :], c.ident[:, :],
                                                start=False, stop=q == TG - 1)
                            ins.then_inc(sum1, 1)
                        if first:
                            i, r, _ = first
                            fg = RING * i + r
                            wait(pe, dist_ready, fg)
                            spread_targets(pe, c, ps_tgt, fg).then_inc(tgt_ready, 1)
                            pe.wait_ge(feat_in[r], (i + 1) * 16)
                            wait(pe, featt_out, fg)
                            pe.sem_inc(begun, 1)
                            for q in range(TG):
                                ins = pe.transpose(ps_featt[0:EF, q * P:(q + 1) * P], feat[r][:, q, :], c.ident[:, :])
                            ins.then_inc(featt_ready, 1)
                        if last:
                            i, r, _ = last
                            pe.wait_ge(gelu2, g + 1)
                            pe.wait_ge(wcol, g + 1)
                            wait(pe, acc_done, g - 1)
                            for q in range(TG):
                                ins = pe.matmul(ps_acc[k][:, 0:MA], hot[r][:, q, :], g2[k][:, q, :],
                                                start=q == 0, stop=q == TG - 1)
                            ins.then_inc(agg_done, 1)
                    pipeline(nc, pe, c, 3, step)

                @block.vector
                def _(ve):
                    for k in range(2):
                        ve.memset(g2[k][:, :, D:D + 1], 1.0).then_inc(ones_set, 1)
                    ve.wait_ge(w_in, 64)

                    def step(stages):
                        last, _, first = stages
                        if last:
                            i, r, b = last
                            g, k = RING * i + r, r % 2
                            wait(ve, agg_done, g - 1)
                            ve.tensor_scalar(g2[k][:, :, D + 1], c.wgt[:, bass.ds(g, 1), :], 1.0, None, ALU.mult) \
                                .then_inc(wcol, 1)
                            ve.wait_ge(sum2, g + 1)
                            wait(ve, gelu2, g)
                            ve.tensor_tensor(u2[:, :, :], ps_2[k][:, :, :], b2r[:, :, :].to_broadcast([P, TG, D]), ALU.add) \
                                .then_inc(biased, 1)
                        if first:
                            i, r, _ = first
                            fg, fk = RING * i + r, r % 2
                            one_hot(ve, c, hot[r], fg).then_inc(hot_ready, 1)
                            ve.wait_ge(featt_ready, fg + 1)
                            wait(ve, sum1, fg - 1)
                            ve.tensor_copy(featt[fk][:, :], ps_featt[0:EF, :]).then_inc(featt_out, 1)
                        if last:
                            ve.wait_ge(agg_done, g + 1)
                            wait(ve, acc_done, g)
                            ve.tensor_tensor(c.acc[:, bass.ds(b, 1), 0:MA], c.acc[:, bass.ds(b, 1), 0:MA],
                                             ps_acc[k][:, 0:MA].unsqueeze(1), ALU.add).then_inc(acc_done, 1)
                    pipeline(nc, ve, c, 3, step)

                @block.scalar
                def _(act):
                    act.wait_ge(w_in, 64)
                    first_idx(act, c, idxb, idx_ready)

                    def step(stages):
                        last, mid, first = stages
                        if last:
                            i, r, _ = last
                            g, k = RING * i + r, r % 2
                            act.wait_ge(biased, g + 1)
                            wait(act, agg_done, g - 1)
                            act.activation(g2[k][:, :, 0:D], u2[:, :, :], ACT.Gelu_apprx_tanh).then_inc(gelu2, 1)
                            next_idx(act, c, idxb, idx_ready, rows_in, i, r)
                        if mid:
                            g, k = RING * mid[0] + mid[1], mid[1] % 2
                            act.wait_ge(sum1, g + 1)
                            wait(act, sum2, g - 1)
                            act.activation(g1[k][:, :], ps_1[k][:, :], ACT.Gelu_apprx_tanh, bias=b1c[:, 0:1]) \
                                .then_inc(gelu1, 1)
                        if first:
                            i, r, _ = first
                            g, k = RING * i + r, r % 2
                            act.wait_ge(tgt_ready, g + 1)
                            wait(act, hott_ready, g)
                            act.activation(dist[:, :], ps_tgt[0:BN, :], ACT.Abs, bias=c.minus_p[0:BN, :]).then_inc(dist_ready, 1)
                            act.wait_ge(dist_ready, g + 1)
                            wait(act, sum1, g - 1)
                            act.activation(hott[k][:, :], dist[:, :], ACT.Relu, bias=c.ones[0:BN, 0:1], scale=-1.0) \
                                .then_inc(hott_ready, 1)
                    pipeline(nc, act, None, 3, step)


HW = HD + 1


def gatv2_pass(nc, c, table, att):
    with ExitStack() as ctx:
        sb, pb = buffers(nc, ctx)
        SC = TG * HEADS
        CUT = SC + HEADS
        rows = [sb(f"rows{r}", [P, TG, D]) for r in range(RING)]
        idxb = [sb(f"idxb{r}", [P, TG], I32) for r in range(RING)]
        hot = [sb(f"hot{r}", [P, TG, BN]) for r in range(RING)]
        hott = [sb(f"hott{r}", [BN, GE], BF16) for r in range(RING)]
        sc = [sb(f"sc{r}", [P, CUT]) for r in range(RING)]
        dist = sb("dist", [BN, GE])
        pen = [sb(f"pen{k}", [BN, GE]) for k in range(2)]
        low = sb("low", [D, GE])
        lr = sb("lr", [D, GE])
        parts = [sb(f"parts{k}", [P, P], BF16) for k in range(2)]
        res = sb("res", [P, CUT])
        srow = sb("srow", [P, P], BF16)
        sel = sb("sel", [P, SC, BN], BF16)
        junk = [sb(f"junk{k}", [BN, GE]) for k in range(2)]
        gtop = sb("gtop", [BN, HEADS])
        old = [sb(f"old{k}", [BN, HEADS]) for k in range(2)]
        drop = [sb(f"drop{k}", [BN, HEADS]) for k in range(2)]
        fade = [sb(f"fade{k}", [BN, HEADS]) for k in range(2)]
        there = sb("there", [P, SC])
        t = sb("t", [P, SC])
        p = [sb(f"p{k}", [P, SC]) for k in range(2)]
        val = [sb(f"val{k}", [P, SC, HW]) for k in range(2)]
        faded = sb("faded", [BN, HEADS, HW])
        attc = sb("attc", [D, 1])
        att4 = sb("att4", [D, HEADS])
        ps_tgt = pb("ps_tgt", [P, 512])
        ps_e = pb("ps_e", [D, 512])
        ps_sc = pb("ps_sc", [P, 512])
        ps_srow = pb("ps_srow", [P, 1024], BF16)
        ps_top = [pb(f"ps_top{k}", [BN, 512]) for k in range(2)]
        ps_node = pb("ps_node", [P, 512])
        ps_acc = pb("ps_acc", [BN, 512])
        with phase(nc, "idx_ready", "in0", "in1", "in2", "in3", "in4", "in5", "in6", "in7", "w_in", "att_set", "att_cols", "sel_set", "cut_set",
                   "tgt_ready", "dist_ready", "hott_ready", "hot_ready", "pen_ready", "sum_e", "low_ready",
                   "lr_ready", "sc_ready", "turned", "hi_out", "sc_out", "res_ready", "mid_out", "lo_out", "srow_ready", "srow_out",
                   "tops", "junked", "node_in", "newtop", "st_done", "drop_ready", "fade_ready", "at_edges",
                   "summed", "t1", "t_ready", "p_ready", "p_in", "val_ready", "agg_done", "faded_ok", "acc_done", "begun") as \
                (idx_ready, in0, in1, in2, in3, in4, in5, in6, in7, w_in, att_set, att_cols, sel_set, cut_set,
                 tgt_ready, dist_ready, hott_ready, hot_ready, pen_ready, sum_e, low_ready,
                 lr_ready, sc_ready, turned, hi_out, sc_out, res_ready, mid_out, lo_out, srow_ready, srow_out,
                 tops, junked, node_in, newtop, st_done, drop_ready, fade_ready, at_edges,
                 summed, t1, t_ready, p_ready, p_in, val_ready, agg_done, faded_ok, acc_done, begun):
            rows_in = (in0, in1, in2, in3, in4, in5, in6, in7)
            with nc.Block() as block:
                @block.gpsimd
                def _(g):
                    g.memset(sel[:, :, :], 0.0).then_inc(sel_set, 1)
                    for m in range(PARTS):
                        g.wait_ge(sel_set, m + 1)
                        g.affine_select(out=sel[:, :, :], in_=sel[:, :, :], compare_op=ALU.not_equal, fill=1.0,
                                        base=-m * CUT, pattern=[[-1, SC], [0, BN]], channel_multiplier=1) \
                            .then_inc(sel_set, 1)
                    gather_rows(g, table, rows, idxb, idx_ready, rows_in, agg_done, begun)

                @block.sync
                def _(sp):
                    with nc.allow_non_contiguous_dma("one column"):
                        sp.dma_start(attc[:, :], att.rearrange("h (f a) -> (h f) a", a=1)).then_inc(w_in, 16)

                @block.vector
                def _(ve):
                    ve.memset(att4[:, :], 0.0).then_inc(att_set, 1)
                    ve.wait_ge(att_set, 1)
                    ve.wait_ge(w_in, 16)
                    for h in range(HEADS):
                        ins = ve.tensor_copy(att4[h * HD:(h + 1) * HD, h:h + 1], attc[h * HD:(h + 1) * HD, :])
                    ins.then_inc(att_cols, 1)
                    for buf in (*sc, *parts):
                        ins = ve.memset(buf[:, :], 0.0)
                    ins.then_inc(cut_set, 1)
                    ve.wait_ge(cut_set, 1)

                    def step(stages):
                        sums, weights, maxima, score, masks = stages
                        if sums:
                            i, r, b = sums
                            g, k = RING * i + r, r % 2
                            ve.wait_ge(rows_in[r], (i + 1) * (16 * TG))
                            ve.wait_ge(p_ready, g + 1)
                            wait(ve, agg_done, g - 1)
                            ve.tensor_tensor(val[k][:, :, 0:HD],
                                             rows[r][:, :, :].rearrange("p q (h f) -> p (q h) f", h=HEADS),
                                             p[k][:, :].unsqueeze(2).to_broadcast([P, SC, HD]), ALU.mult).then_inc(p_in, 1)
                            ve.tensor_copy(val[k][:, :, HD], p[k][:, :]).then_inc(val_ready, 1)
                            ve.wait_ge(fade_ready, g + 1)
                            wait(ve, acc_done, g)
                            ve.tensor_tensor(faded[:, :, :], c.acc[:, bass.ds(b, 1), 0:HEADS * HW]
                                             .rearrange("p a (h f) -> p (a h) f", h=HEADS),
                                             fade[k][:, :].unsqueeze(2).to_broadcast([BN, HEADS, HW]), ALU.mult) \
                                .then_inc(faded_ok, 1)
                        if weights:
                            wi, wr, _ = weights
                            wg = RING * wi + wr
                            ve.wait_ge(at_edges, wg + 1)
                            ve.tensor_reduce(there[:, :].rearrange("p (q h) -> p q h", q=TG),
                                             ps_node[:, 0:PARTS * SC].rearrange("p (q m h) -> p q h m", q=TG, m=PARTS),
                                             AX.X, ALU.add).then_inc(summed, 1)
                            ve.wait_ge(summed, wg + 1)
                            ve.tensor_tensor(t[:, :], sc[wr][:, 0:SC], there[:, :], ALU.subtract).then_inc(t1, 1)
                            ve.wait_ge(t1, wg + 1)
                            ve.tensor_scalar(t[:, :], t[:, :], 0.0, None, ALU.min).then_inc(t_ready, 1)
                        if score:
                            si, sr, _ = score
                            sg = RING * si + sr
                            ve.wait_ge(low_ready, sg + 1)
                            wait(ve, sc_ready, sg)
                            ve.tensor_tensor(lr[:, :], low[:, :], ps_e[:, :], ALU.max).then_inc(lr_ready, 1)
                        if maxima:
                            mi, mr, mb = maxima
                            mg, mk = RING * mi + mr, mr % 2
                            wait(ve, st_done, mg)
                            ve.tensor_scalar(old[mk][:, :], c.top[:, bass.ds(mb, 1), :], 1.0, None, ALU.mult).then_inc(node_in, 1)
                            ve.wait_ge(pen_ready, mg + 1)
                            wait(ve, newtop, mg)
                            for h in range(HEADS):
                                ve.wait_ge(tops, HEADS * mg + (h + 1))
                                wait(ve, junked, HEADS * mg + (h - 1))
                                ve.sem_inc(begun, 1)
                                ve.tensor_tensor_reduce(out=junk[h % 2][:, :], in0=pen[mk][:, :], in1=ps_top[h % 2][:, :],
                                                        scale=1.0, scalar=-BIG, op0=ALU.add, op1=ALU.max,
                                                        accum_out=gtop[:, h:h + 1]).then_inc(junked, 1)
                            ve.wait_ge(node_in, mg + 1)
                            ve.wait_ge(junked, HEADS * mg + HEADS)
                            newr = (mr + 1) % RING
                            new = sc[newr][0:BN, SC:CUT]
                            ve.tensor_tensor(new, old[mk][:, :], gtop[:, :], ALU.max).then_inc(newtop, 1)
                        if sums:
                            ve.wait_ge(agg_done, g + 1)
                            ve.wait_ge(faded_ok, g + 1)
                            ve.tensor_tensor(c.acc[:, bass.ds(b, 1), 0:HEADS * HW],
                                             faded[:, :, :].rearrange("p h f -> p (h f)").unsqueeze(1),
                                             ps_acc[:, 0:HEADS * HW].unsqueeze(1), ALU.add).then_inc(acc_done, 1)
                        if score:
                            ve.wait_ge(sc_out, sg + 1)
                        if maxima:
                            ve.wait_ge(newtop, mg + 1)
                        if score or maxima:
                            cr = sr if score else newr
                            n = sg if score else mg + 1
                            ck = cr % 2
                            wait(ve, srow_ready, n - 1)
                            wait(ve, at_edges, n - 2)
                            hi, mid, lo = (parts[ck][:, m * CUT:(m + 1) * CUT] for m in range(PARTS))
                            ve.tensor_copy(hi, sc[cr][:, :]).then_inc(hi_out, 1)
                        if maxima:
                            ve.tensor_scalar(c.top[:, bass.ds(mb, 1), :], new, 1.0, None, ALU.mult).then_inc(st_done, 1)
                        if score or maxima:
                            ve.wait_ge(hi_out, n + 1)
                            wait(ve, lo_out, n)
                            ve.tensor_tensor(res[:, :], sc[cr][:, :], hi, ALU.subtract).then_inc(res_ready, 1)
                        if maxima:
                            ve.tensor_tensor(drop[mk][:, :], old[mk][:, :], new, ALU.subtract).then_inc(drop_ready, 1)
                        if score or maxima:
                            ve.wait_ge(res_ready, n + 1)
                            ve.tensor_copy(mid, res[:, :]).then_inc(mid_out, 1)
                            ve.wait_ge(mid_out, n + 1)
                            ve.tensor_tensor(lo, res[:, :], mid, ALU.subtract).then_inc(lo_out, 1)
                    pipeline(nc, ve, c, 5, step)

                @block.scalar
                def _(act):
                    act.wait_ge(cut_set, 1)
                    first_idx(act, c, idxb, idx_ready)

                    def step(stages):
                        sums, weights, maxima, score, masks = stages
                        if masks:
                            fi, fr, _ = masks
                            fg = RING * fi + fr
                            act.wait_ge(tgt_ready, fg + 1)
                            wait(act, hott_ready, fg)
                            act.activation(dist[:, :], ps_tgt[0:BN, :], ACT.Abs, bias=c.minus_p[0:BN, :]).then_inc(dist_ready, 1)
                        if maxima:
                            mg = RING * maxima[0] + maxima[1]
                            act.wait_ge(srow_ready, mg + 1)
                            wait(act, tops, HEADS * mg)
                            act.activation(srow[:, :], ps_srow[:, 0:P], ACT.Copy).then_inc(srow_out, 1)
                        if score:
                            si, sr, _ = score
                            sg, sk = RING * si + sr, sr % 2
                            act.wait_ge(sum_e, sg + 1)
                            wait(act, lr_ready, sg)
                            act.activation(low[:, :], ps_e[:, :], ACT.Copy, scale=0.2).then_inc(low_ready, 1)
                        if score:
                            act.wait_ge(turned, sg + 1)
                            act.activation(hot[sr][:, :, :], ps_srow[:, P:(TG + 1) * P].rearrange("p (q n) -> p q n", q=TG)[:, :, 0:BN],
                                           ACT.Copy).then_inc(hot_ready, 1)
                        if weights:
                            i, r, _ = weights
                            g, k = RING * i + r, r % 2
                            act.wait_ge(t_ready, g + 1)
                            wait(act, val_ready, g - 1)
                            act.activation(p[k][:, :], t[:, :], ACT.Exp).then_inc(p_ready, 1)
                            act.wait_ge(drop_ready, g + 1)
                            wait(act, faded_ok, g - 1)
                            act.activation(fade[k][:, :], drop[k][:, :], ACT.Exp).then_inc(fade_ready, 1)
                        if masks:
                            act.wait_ge(dist_ready, fg + 1)
                            act.activation(hott[fr][:, :], dist[:, :], ACT.Relu, bias=c.ones[0:BN, 0:1], scale=-1.0) \
                                .then_inc(hott_ready, 1)
                        if score:
                            act.wait_ge(hott_ready, sg + 1)
                            wait(act, junked, HEADS * sg - HEADS)
                            act.activation(pen[sk][:, :], hott[sr][:, :], ACT.Copy, bias=-BIG, scale=BIG).then_inc(pen_ready, 1)
                            act.wait_ge(sc_ready, sg + 1)
                            act.activation(sc[sr][:, 0:SC], ps_sc[:, 0:SC], ACT.Copy).then_inc(sc_out, 1)
                        if sums:
                            next_idx(act, c, idxb, idx_ready, rows_in, sums[0], sums[1])
                    pipeline(nc, act, None, 5, step)

                @block.tensor
                def _(pe):
                    pe.wait_ge(att_cols, 1)
                    pe.wait_ge(sel_set, 1 + PARTS)

                    def step(stages):
                        sums, weights, maxima, score, masks = stages
                        if masks:
                            fg = RING * masks[0] + masks[1]
                            wait(pe, dist_ready, fg)
                            spread_targets(pe, c, ps_tgt, fg).then_inc(tgt_ready, 1)
                        if score:
                            i, r, b = score
                            sg = RING * i + r
                            pe.wait_ge(hott_ready, sg + 1)
                            wait(pe, lr_ready, sg)
                            for m in range(PARTS):
                                pe.matmul(ps_e[:, :], c.mine[:, bass.ds(b, 1), m, :].rearrange("p a f -> p (a f)"),
                                          hott[r][:, :], start=m == 0, stop=False)
                            pe.wait_ge(rows_in[r], (i + 1) * (16 * TG))
                            for q in range(TG):
                                ins = pe.matmul(ps_e[:, q * P:(q + 1) * P], rows[r][:, q, :], c.ident[:, :],
                                                start=False, stop=q == TG - 1)
                            ins.then_inc(sum_e, 1)
                        if score:
                            wait(pe, hot_ready, sg)
                            wait(pe, srow_out, sg - 1)
                            pe.sem_inc(begun, 1)
                            for q in range(TG):
                                ins = pe.transpose(ps_srow[:, (q + 1) * P:(q + 1) * P + BN], hott[r][:, q * P:(q + 1) * P],
                                                   c.identb[0:BN, 0:BN])
                            ins.then_inc(turned, 1)
                        if maxima:
                            mg, mk = RING * maxima[0] + maxima[1], maxima[1] % 2
                            pe.wait_ge(lo_out, mg + 1)
                            wait(pe, srow_out, mg)
                            wait(pe, hot_ready, mg)
                            pe.sem_inc(begun, 1)
                            pe.transpose(ps_srow[:, 0:P], parts[mk][:, :], c.identb[:, :]).then_inc(srow_ready, 1)
                        if weights:
                            i, r, _ = weights
                            g, k = RING * i + r, (r + 1) % 2
                            pe.wait_ge(lo_out, g + 2)
                            wait(pe, summed, g)
                            maxima_parts = parts[k][0:BN, 0:PARTS * CUT].rearrange("p (m j) -> p m j", m=PARTS)[:, :, SC:CUT]
                            for q in range(TG):
                                ins = pe.matmul(ps_node[:, q * PARTS * HEADS:(q + 1) * PARTS * HEADS]
                                                .rearrange("p (m h) -> p m h", m=PARTS),
                                                hott[r][:, q * P:(q + 1) * P], maxima_parts, start=True, stop=True)
                            ins.then_inc(at_edges, 1)
                        def spread_scores(heads):
                            for h in heads:
                                wait(pe, junked, HEADS * mg + (h - 1))
                                for q in range(TG):
                                    ins = pe.matmul(ps_top[h % 2][:, q * P:(q + 1) * P], sel[:, q * HEADS + h, :],
                                                    srow[:, :], start=True, stop=True)
                                ins.then_inc(tops, 1)
                        if maxima:
                            pe.wait_ge(srow_out, mg + 1)
                            spread_scores((0, 1))
                        if sums:
                            i, r, _ = sums
                            g, k = RING * i + r, r % 2
                            pe.wait_ge(hot_ready, g + 1)
                            pe.wait_ge(val_ready, g + 1)
                            pe.wait_ge(p_in, g + 1)
                            wait(pe, acc_done, g)
                            for q in range(TG):
                                ins = pe.matmul(ps_acc[:, 0:HEADS * HW], hot[r][:, q, :],
                                                val[k][:, q * HEADS:(q + 1) * HEADS, :].rearrange("p h f -> p (h f)"),
                                                start=q == 0, stop=q == TG - 1)
                            ins.then_inc(agg_done, 1)
                        if score:
                            pe.wait_ge(lr_ready, sg + 1)
                            wait(pe, sc_out, sg)
                            for q in range(TG):
                                ins = pe.matmul(ps_sc[:, q * HEADS:(q + 1) * HEADS], lr[:, q * P:(q + 1) * P],
                                                att4[:, :], start=True, stop=True)
                            ins.then_inc(sc_ready, 1)
                        if maxima:
                            spread_scores((2, 3))
                    pipeline(nc, pe, c, 5, step)


def gcn_pass(nc, c, table):
    with ExitStack() as ctx:
        sb, pb = buffers(nc, ctx)
        rows = [sb(f"rows{r}", [P, TG, D]) for r in range(RING)]
        idxb = [sb(f"idxb{r}", [P, TG], I32) for r in range(RING)]
        hot = [sb(f"hot{k}", [P, TG, BN]) for k in range(2)]
        ps_acc = [pb(f"ps_acc{k}", [BN, 512]) for k in range(2)]
        with phase(nc, "idx_ready", "in0", "in1", "in2", "in3", "in4", "in5", "in6", "in7", "hot_ready", "agg_done", "acc_done", "begun") as \
                (idx_ready, in0, in1, in2, in3, in4, in5, in6, in7, hot_ready, agg_done, acc_done, begun):
            rows_in = (in0, in1, in2, in3, in4, in5, in6, in7)
            with nc.Block() as block:
                @block.gpsimd
                def _(g):
                    gather_rows(g, table, rows, idxb, idx_ready, rows_in, agg_done, begun)

                @block.scalar
                def _(act):
                    first_idx(act, c, idxb, idx_ready)

                    def step(stages):
                        if stages[0]:
                            next_idx(act, c, idxb, idx_ready, rows_in, *stages[0][0:2])
                    pipeline(nc, act, None, 2, step)

                @block.vector
                def _(ve):
                    def step(stages):
                        last, first = stages
                        if first:
                            i, r, _ = first
                            fg, fk = RING * i + r, r % 2
                            wait(ve, agg_done, fg - 1)
                            one_hot(ve, c, hot[fk], fg, lambda q: c.wgt[:, bass.ds(fg, 1), q]).then_inc(hot_ready, 1)
                        if last:
                            i, r, b = last
                            g, k = RING * i + r, r % 2
                            ve.wait_ge(agg_done, g + 1)
                            wait(ve, acc_done, g)
                            ve.tensor_tensor(c.acc[:, bass.ds(b, 1), 0:D], c.acc[:, bass.ds(b, 1), 0:D],
                                             ps_acc[k][:, 0:D].unsqueeze(1), ALU.add).then_inc(acc_done, 1)
                    pipeline(nc, ve, c, 2, step)

                @block.tensor
                def _(pe):
                    def step(stages):
                        if stages[0]:
                            i, r, _ = stages[0]
                            g, k = RING * i + r, r % 2
                            pe.wait_ge(rows_in[r], (i + 1) * (16 * TG))
                            pe.wait_ge(hot_ready, g + 1)
                            wait(pe, acc_done, g - 1)
                            for q in range(TG):
                                ins = pe.matmul(ps_acc[k][:, 0:D], hot[k][:, q, :], rows[r][:, q, :],
                                                start=q == 0, stop=q == TG - 1)
                            ins.then_inc(agg_done, 1)
                    pipeline(nc, pe, None, 2, step)


def cut_rows(ve, step, c, rows):
    hi, mid, lo = (c.mine[:, :, m, :] for m in range(PARTS))
    step(ve.tensor_copy(hi, rows))
    step(ve.tensor_tensor(c.other[:, :, :], rows, hi, ALU.subtract))
    step(ve.tensor_copy(mid, c.other[:, :, :]))
    step(ve.tensor_tensor(lo, c.other[:, :, :], mid, ALU.subtract))


def vector_steps(nc, build):
    with phase(nc, "v") as (v,):
        with nc.Block() as block:
            @block.vector
            def _(ve):
                build(ve, chained(ve, v))


def gnn_kernel(nc, a, out):
    c = Chip()
    dram = lambda name, rows, cols: nc.dram_tensor(name, (rows, cols), F32, kind="Internal").ap()
    recs = dram("records", SLOTS, REC)
    gat_tab = dram("gat_table", N, GW)
    src_tab = dram("source_table", N, D)
    nodes = lambda ap: ap.rearrange("(b p) f -> p b f", p=BN)
    full = [BN, NB, D]
    with ExitStack() as ctx:
        sb, pb = buffers(nc, ctx)
        c.x = sb("x", full)
        c.h = sb("h", full)
        c.idx = sb("idx", [P, NG + RING, TG], I32)
        c.dlo = sb("dlo", [P, NG, TG])
        c.dlob = sb("dlob", [P, NG, TG], BF16)
        c.wgt = sb("wgt", [P, NG, TG])
        c.gblk = sb("gblk", [1, NG], I32)
        c.iota = sb("iota", [P, BN])
        c.ident = sb("ident", [P, P])
        c.identb = sb("identb", [P, P], BF16)
        c.minus_p = sb("minus_p", [P, 1])
        c.ones = sb("ones_pp", [P, P])
        c.acc = sb("acc", [BN, NB, GW])
        c.st = sb("st", [BN, NB, 2])
        c.deg = sb("deg", [BN, NB])
        c.other = sb("other", full)

        sort_edges(nc, c, a["src"], a["dst"], a["edge_weight"], a["edge_attr_64"], recs)
        load_meta(nc, c, recs)
        load_rows(nc, [(c.x[:, :, :], nodes(a["x"]))])

        normalise(nc, c, c.x, c.h)
        with ExitStack() as layer:
            c.rows = buffers(nc, layer)[0]("rows", [BN, NB, GW])
            for l in range(3):
                gat_tables(nc, c, c.h, a["L0_gnn_W"][l], a["L0_gnn_a_src"][l], a["L0_gnn_a_dst"][l], gat_tab)
                gat_pass(nc, c, gat_tab)
                gat_norm(nc, c, a["L0_gnn_b"][l], c.h, add_to=c.x if l == 2 else None)

        normalise(nc, c, c.x, c.h)
        with ExitStack() as layer:
            lb = buffers(nc, layer)[0]
            w = lb("w", [D, 7, D])
            brow = lb("brow", [BN, 3, D])
            rows2 = lb("rows2", [BN, NB, 2 * D])
            c.mine = lb("mine", [BN, NB, PARTS, D], BF16)
            agg = lb("agg", full)
            add = lb("add", full)
            cnt = lb("cnt", [BN, 2, NB])
            load_rows(nc, [(w[:, 0, :], a["L1_gnn_mW1"][0:D, :]), (w[:, 1, :], a["L1_gnn_mW1"][D:2 * D, :]),
                           (w[:, 2, :], a["L1_gnn_mW3"]), (w[:, 3, :], a["L1_gnn_uW1"][0:D, :]),
                           (w[:, 4, :], a["L1_gnn_uW1"][D:2 * D, :]), (w[:, 5, :], a["L1_gnn_uW2"]),
                           (brow[:, 0, :], a["L1_gnn_mb3"].partition_broadcast(BN)),
                           (brow[:, 1, :], a["L1_gnn_ub1"].partition_broadcast(BN)),
                           (brow[:, 2, :], a["L1_gnn_ub2"].partition_broadcast(BN))])
            linear(nc, c, [(c.h, w[:, 0:2, :].rearrange("p a f -> p (a f)"))], 2 * D, rows2, table=src_tab, table_cols=D)

            def before(ve, step):
                cut_rows(ve, step, c, rows2[:, :, D:2 * D])
                step(ve.memset(c.acc[:, :, :], 0.0))
            vector_steps(nc, before)
            mlp_pass(nc, c, src_tab, recs, a["L1_gnn_mW1"], a["L1_gnn_mb1"], a["L1_gnn_mW2"], a["L1_gnn_mb2"])

            def mean(ve, step):
                step(ve.tensor_copy(c.deg[:, :], c.acc[:, :, D + 1]))
                step(ve.tensor_scalar(cnt[:, 0, :], c.acc[:, :, D], 1e-8, None, ALU.add))
                step(ve.reciprocal(cnt[:, 0, :], cnt[:, 0, :]))
                step(ve.tensor_tensor(cnt[:, 1, :], c.acc[:, :, D], cnt[:, 0, :], ALU.mult))
                step(ve.tensor_tensor(agg[:, :, :], c.acc[:, :, 0:D], cnt[:, 0, :].unsqueeze(2).to_broadcast(full), ALU.mult))
                step(ve.tensor_copy(add[:, :, :], brow[:, 0:1, :].to_broadcast(full)))
                step(ve.tensor_tensor(add[:, :, :], add[:, :, :], cnt[:, 1, :].unsqueeze(2).to_broadcast(full), ALU.mult))
            vector_steps(nc, mean)
            linear(nc, c, [(agg, w[:, 2, :])], D, c.other, addend=lambda b: add[:, b, :])
            linear(nc, c, [(c.h, w[:, 3, :]), (c.other, w[:, 4, :])], D, agg, addend=lambda b: brow[:, 1, :],
                   func=ACT.Gelu_apprx_tanh)

            def residual(ve, step):
                step(ve.tensor_tensor(add[:, :, :], c.h[:, :, :], brow[:, 2:3, :].to_broadcast(full), ALU.add))
            vector_steps(nc, residual)
            linear(nc, c, [(agg, w[:, 5, :])], D, c.other, addend=lambda b: add[:, b, :])
        normalise(nc, c, c.other, None, relu=False, scale=a["L1_gnn_gamma"], shift=a["L1_gnn_beta"], add_to=c.x)

        normalise(nc, c, c.x, c.h)
        with ExitStack() as layer:
            lb = buffers(nc, layer)[0]
            w = lb("w", [D, 2 * D])
            brow = lb("brow", [BN, 2, D])
            rows2 = lb("rows2", [BN, NB, 2 * D])
            c.mine = lb("mine", [BN, NB, PARTS, D], BF16)
            bias = lb("bias", [BN, 1, D])
            den = lb("den", [BN, NB, HEADS])
            c.top = lb("top", [BN, NB, HEADS])
            for l in ("0", "1"):
                load_rows(nc, [(w[:, 0:D], a["L2_gnn_Wl" + l]), (w[:, D:2 * D], a["L2_gnn_Wr" + l]),
                               (brow[:, 0, :], a["L2_gnn_bl" + l].partition_broadcast(BN)),
                               (brow[:, 1, :], a["L2_gnn_br" + l].partition_broadcast(BN)),
                               (bias[:, 0, :], a["L2_gnn_bias" + l].partition_broadcast(BN))])
                linear(nc, c, [(c.h, w[:, :])], 2 * D, rows2, addend=lambda b: brow[:, :, :].rearrange("p a f -> p (a f)"),
                       table=src_tab, table_cols=D)

                def before(ve, step):
                    cut_rows(ve, step, c, rows2[:, :, D:2 * D])
                    step(ve.memset(c.acc[:, :, :], 0.0))
                    step(ve.memset(c.top[:, :, :], -BIG))
                vector_steps(nc, before)
                gatv2_pass(nc, c, src_tab, a["L2_gnn_att" + l])

                def divide(ve, step):
                    heads = c.acc[:, :, 0:HEADS * HW].rearrange("p b (h f) -> p b h f", h=HEADS)
                    step(ve.tensor_scalar(den[:, :, :], heads[:, :, :, HD], 1e-16, None, ALU.add))
                    step(ve.reciprocal(den[:, :, :], den[:, :, :]))
                    for h in range(HEADS):
                        step(ve.tensor_tensor(c.other[:, :, h * HD:(h + 1) * HD], c.acc[:, :, h * HW:h * HW + HD],
                                              den[:, :, h:h + 1].to_broadcast([BN, NB, HD]), ALU.mult))
                    step(ve.tensor_tensor(c.other[:, :, :], c.other[:, :, :], bias[:, :, :].to_broadcast(full), ALU.add))
                vector_steps(nc, divide)
                normalise(nc, c, c.other, c.h, relu=False, scale=a["L2_gnn_g" + l], shift=a["L2_gnn_b" + l], elu=True,
                          add_to=c.x if l == "1" else None)

        normalise(nc, c, c.x, c.h)
        with ExitStack() as layer:
            lb = buffers(nc, layer)[0]
            w = lb("w", [D, 2, D])
            bias = lb("bias", [BN, 2, D])
            dinv = lb("dinv", [BN, NB])
            has = lb("has", [BN, NB])
            load_rows(nc, [(w[:, 0, :], a["L3_gnn_W1"]), (w[:, 1, :], a["L3_gnn_W2"]),
                           (bias[:, 0, :], a["L3_gnn_b1"].partition_broadcast(BN)),
                           (bias[:, 1, :], a["L3_gnn_b2"].partition_broadcast(BN))])
            with phase(nc, "v", "deg_ready", "root_ready") as (v, deg_ready, root_ready):
                with nc.Block() as block:
                    @block.vector
                    def _(ve):
                        step = chained(ve, v)
                        step(ve.tensor_scalar(has[:, :], c.deg[:, :], 0.0, None, ALU.is_gt))
                        ve.tensor_scalar(dinv[:, :], c.deg[:, :], 1e-12, None, ALU.max).then_inc(deg_ready, 1)
                        ve.wait_ge(root_ready, 1)
                        step(ve.reciprocal(dinv[:, :], dinv[:, :]))
                        step(ve.tensor_tensor(dinv[:, :], dinv[:, :], has[:, :], ALU.mult))

                    @block.scalar
                    def _(act):
                        act.wait_ge(deg_ready, 1)
                        act.activation(dinv[:, :], dinv[:, :], ACT.Sqrt).then_inc(root_ready, 1)
            for l in range(2):
                linear(nc, c, [(c.h, w[:, l, :])], D, c.other, row_scale=lambda b: dinv[:, b:b + 1],
                       table=src_tab, table_cols=D)
                vector_steps(nc, lambda ve, step: step(ve.memset(c.acc[:, :, :], 0.0)))
                gcn_pass(nc, c, src_tab)

                def after(ve, step):
                    step(ve.tensor_tensor(c.other[:, :, :], c.acc[:, :, 0:D], dinv[:, :].unsqueeze(2).to_broadcast(full), ALU.mult))
                    step(ve.tensor_tensor(c.other[:, :, :], c.other[:, :, :], bias[:, l:l + 1, :].to_broadcast(full), ALU.add))
                vector_steps(nc, after)
                n = str(l + 1)
                normalise(nc, c, c.other, c.h, scale=a["L3_gnn_g" + n], shift=a["L3_gnn_be" + n],
                          add_to=c.x if l == 1 else None)

        with phase(nc, "stored") as (stored,):
            with nc.Block() as block:
                @block.sync
                def _(sp):
                    sp.dma_start(nodes(out), c.x[:, :, :]).then_inc(stored, 16)
                    sp.wait_ge(stored, 16)


def kernel(**inputs):
    import numpy as _np
    import concourse.bacc as _bacc
    from concourse import mybir as _mybir
    from concourse.bass_utils import run_bass_kernel_spmd as _run

    nc = _bacc.Bacc("TRN2", target_bir_lowering=False, num_devices=1)
    arrays, args = {}, {}
    for name, value in inputs.items():
        a = _np.ascontiguousarray(value)
        arrays[f"in_{name}_dram"] = a
        args[name] = nc.dram_tensor(f"in_{name}_dram", a.shape, _mybir.dt.from_np(a.dtype), kind="ExternalInput").ap()
    out = nc.dram_tensor("out_0_dram", (N, D), _mybir.dt.float32, kind="ExternalOutput").ap()
    gnn_kernel(nc, args, out)
    r = _run(nc, [arrays], core_ids=[0])
    return r.results[0]["out_0_dram"]
```
